# Optimizing a Trainium2 kernel written in Bass

```python
import numpy as np
import jax
import jax.numpy as jnp

def _softmax(x, axis=-1):
    return jax.nn.softmax(x, axis=axis)

def _gelu(x):
    return jax.nn.gelu(x, approximate=True)

def _silu(x):
    return jax.nn.silu(x)

def _sigmoid(x):
    return jax.nn.sigmoid(x)

def _layernorm(x, axis=-1, eps=1e-05):
    m = jnp.mean(x, axis=axis, keepdims=True)
    v = jnp.var(x, axis=axis, keepdims=True)
    return (x - m) / jnp.sqrt(v + eps)

def _scatter_add(tgt, idx, src, axis=0):
    return tgt.at[idx].add(src)

def _segment_sum(src, seg, n):
    return jax.ops.segment_sum(src, seg, n)
kernel_name = 'mk_macaron_d2_jaxref_r8_bc59e0'

def setup_inputs(seed: int=0):
    np.random.seed(seed)
    _w = jnp.asarray

    def _L0_attn_setup():
        import jax, jax.numpy as jnp
        import numpy as np
        B, T, W, H = (8, 512, 128, 8)
        BW = W // H

        def _bdl(x, w, b):
            xh = x.reshape(x.shape[:-1] + (H, BW))
            y = jnp.einsum('bthi,hij->bthj', xh, w) + b
            return y.reshape(x.shape)
        key = jax.random.key(seed)
        ks = jax.random.split(key, 6)
        x = jax.random.normal(ks[0], (B, T, W), dtype=jnp.float32)
        std = 1.0 / np.sqrt(BW)
        w_in = jax.random.normal(ks[1], (H, BW, BW), dtype=jnp.float32) * std
        b_in = jnp.zeros((H, BW), dtype=jnp.float32)
        w_a = jax.random.normal(ks[2], (H, BW, BW), dtype=jnp.float32) * std
        b_a = jnp.zeros((H, BW), dtype=jnp.float32)
        eps = 1e-08
        u = jax.random.uniform(ks[3], (W,), minval=0.9 ** 2 + eps, maxval=0.999 ** 2 + eps)
        t = 0.5 * jnp.log(u)
        a_param = jnp.log(jnp.exp(-t) - 1.0).astype(jnp.float32)
        return {'x': x, 'w_in': w_in, 'b_in': b_in, 'w_a': w_a, 'b_a': b_a, 'a_param': a_param}
    _L0_attn_in = _L0_attn_setup()

    def _L0_ffn_setup():
        import jax, jax.numpy as jnp
        import numpy as np
        HIDDEN = 128
        FFN = 512
        N_EXPERTS = 8
        TOP_K = 2
        key = jax.random.key(seed)
        ks = jax.random.split(key, 6)
        x = jax.random.normal(ks[0], (2, 256, HIDDEN), dtype=jnp.float32)
        Wr = jax.random.normal(ks[1], (N_EXPERTS, HIDDEN), dtype=jnp.float32) * 0.02
        W1 = jax.random.normal(ks[2], (N_EXPERTS, FFN, HIDDEN), dtype=jnp.float32) * 0.02
        b1 = jnp.zeros((N_EXPERTS, FFN), dtype=jnp.float32)
        W2 = jax.random.normal(ks[3], (N_EXPERTS, HIDDEN, FFN), dtype=jnp.float32) * 0.02
        b2 = jnp.zeros((N_EXPERTS, HIDDEN), dtype=jnp.float32)
        return {'x': x, 'Wr': Wr, 'W1': W1, 'b1': b1, 'W2': W2, 'b2': b2}
    _L0_ffn_in = _L0_ffn_setup()

    def _L1_attn_setup():
        import jax, jax.numpy as jnp
        import numpy as np
        INIT_L = 512.0
        EPS = 1e-06
        N_HEAD = 16

        def fire_bias(T, w1, b1, w2, b2, c, L_multiplier):
            pos = jnp.arange(T, dtype=jnp.float32)
            rel = pos[:, None] - pos[None, :]
            threshold = jnp.abs(L_multiplier * INIT_L)
            pos_norm = jnp.maximum(pos, threshold)[:, None]
            rel = jnp.log(jnp.abs(c * rel) + 1.0)
            pos_norm = jnp.log(jnp.abs(c * pos_norm) + 1.0) + EPS
            nd = rel / pos_norm
            h = jax.nn.relu(nd[..., None] * w1[0] + b1)
            bias = jnp.einsum('tsw,wh->hts', h, w2) + b2[:, None, None]
            causal = jnp.tril(jnp.ones((T, T), dtype=bool))
            bias = jnp.where(causal[None], bias, -jnp.inf)
            return bias[None]
        key = jax.random.key(seed)
        ks = jax.random.split(key, 8)
        B, T, C, H, W = (2, 256, 128, 16, 32)
        s = 0.02
        return {'x': jax.random.normal(ks[0], (B, T, C), jnp.float32), 'Wqkv': jax.random.normal(ks[1], (C, 3 * C), jnp.float32) * s, 'bqkv': jnp.zeros((3 * C,), jnp.float32), 'Wproj': jax.random.normal(ks[2], (C, C), jnp.float32) * s, 'bproj': jnp.zeros((C,), jnp.float32), 'w1': jax.random.normal(ks[3], (1, W), jnp.float32), 'b1': jnp.zeros((W,), jnp.float32), 'w2': jax.random.normal(ks[4], (W, H), jnp.float32) * 0.1, 'b2': jnp.zeros((H,), jnp.float32), 'c_param': jnp.float32(0.1), 'L_multiplier': jnp.float32(1.0)}
    _L1_attn_in = _L1_attn_setup()

    def _L1_ffn_setup():
        import jax, jax.numpy as jnp
        import numpy as np
        DIM = 128
        DEPTH = 6
        HEADS = 16
        DIM_HEAD = 64
        WINDOW = 32
        INNER = HEADS * DIM_HEAD
        DIM_INNER = int(DIM * 4 * 2 / 3)
        QK_SCALE = 8.0

        def shift_tokens(t):
            a, s = jnp.split(t, 2, -1)
            s = jnp.pad(s, ((0, 0), (1, 0), (0, 0)))[:, :-1]
            return jnp.concatenate([a, s], -1)

        def l2norm(t):
            return t / jnp.maximum(jnp.linalg.norm(t, axis=-1, keepdims=True), 1e-12)

        def rotate_half(x):
            x1, x2 = jnp.split(x, 2, -1)
            return jnp.concatenate([-x2, x1], -1)

        def rotary_tables(n):
            half = jnp.arange(0, DIM_HEAD, 2, dtype=jnp.float32)
            inv_freq = 1.0 / 10000.0 ** (half / DIM_HEAD)
            t = jnp.arange(n, dtype=jnp.float32)
            freqs = t[:, None] * inv_freq[None, :]
            freqs = jnp.concatenate([freqs, freqs], -1)
            base_scale = (half + 0.4 * DIM_HEAD) / (1.4 * DIM_HEAD)
            power = (t - n // 2) / (WINDOW // 2)
            scale = base_scale[None, :] ** power[:, None]
            scale = jnp.concatenate([scale, scale], -1)
            return (freqs, scale)

        def local_attention(q, k, v):
            b, h, n, d = q.shape
            w = WINDOW
            nw = n // w
            bq = q.reshape(b, h, nw, w, d)
            bk = k.reshape(b, h, nw, w, d)
            bv = v.reshape(b, h, nw, w, d)

            def look(t):
                p = jnp.pad(t, ((0, 0), (0, 0), (1, 0), (0, 0), (0, 0)))
                return jnp.concatenate([p[:, :, :nw], p[:, :, 1:]], axis=3)
            bk2, bv2 = (look(bk), look(bv))
            seq = jnp.arange(n).reshape(nw, w)
            seq_p = jnp.pad(seq, ((1, 0), (0, 0)), constant_values=-1)
            jt = jnp.concatenate([seq_p[:nw], seq_p[1:]], axis=1)
            it = seq[:, :, None]
            jb = jt[:, None, :]
            mask = (it < jb) | (it > jb + w) | (jb == -1)
            sim = jnp.einsum('bhwie,bhwje->bhwij', bq, bk2) * QK_SCALE
            sim = jnp.where(mask, -jnp.finfo(sim.dtype).max, sim)
            attn = jax.nn.softmax(sim, -1)
            out = jnp.einsum('bhwij,bhwje->bhwie', attn, bv2)
            return out.reshape(b, h, n, d)

        def attn_layer(x, Wqkv, qs, ksc, Wo):
            b, n, _ = x.shape
            qkv = x @ Wqkv
            q, k, v = jnp.split(qkv, 3, -1)
            sh = lambda t: t.reshape(b, n, HEADS, DIM_HEAD).transpose(0, 2, 1, 3)
            q, k, v = (sh(q), sh(k), sh(v))
            q = l2norm(q) * qs
            k = l2norm(k) * ksc
            freqs, scale = rotary_tables(n)
            cos, sin = (jnp.cos(freqs), jnp.sin(freqs))
            q = q * cos * scale + rotate_half(q) * sin * scale
            inv = 1.0 / scale
            k = k * cos * inv + rotate_half(k) * sin * inv
            out = local_attention(q, k, v)
            out = out.transpose(0, 2, 1, 3).reshape(b, n, INNER)
            return out @ Wo

        def ffn_layer(x, g, bln, W1, b1, W2, b2):
            mu = x.mean(-1, keepdims=True)
            var = ((x - mu) ** 2).mean(-1, keepdims=True)
            xn = (x - mu) / jnp.sqrt(var + 1e-05) * g + bln
            hg = xn @ W1 + b1
            a, gate = jnp.split(hg, 2, -1)
            return a * jax.nn.gelu(gate, approximate=False) @ W2 + b2
        key = jax.random.key(seed)
        ks = jax.random.split(key, 8)
        B, N = (2, 256)
        init = lambda k, shape: jax.random.normal(k, shape, jnp.float32) * 0.02
        return {'x': jax.random.normal(ks[0], (B, N, DIM), jnp.float32), 'Wqkv': init(ks[1], (DEPTH, DIM, 3 * INNER)), 'q_scale': jnp.ones((DEPTH, DIM_HEAD), jnp.float32), 'k_scale': jnp.ones((DEPTH, DIM_HEAD), jnp.float32), 'Wo': init(ks[2], (DEPTH, INNER, DIM)), 'ln_g': jnp.ones((DEPTH, DIM), jnp.float32), 'ln_b': jnp.zeros((DEPTH, DIM), jnp.float32), 'W1': init(ks[3], (DEPTH, DIM, 2 * DIM_INNER)), 'b1': jnp.zeros((DEPTH, 2 * DIM_INNER), jnp.float32), 'W2': init(ks[4], (DEPTH, DIM_INNER, DIM)), 'b2': jnp.zeros((DEPTH, DIM), jnp.float32)}
    _L1_ffn_in = _L1_ffn_setup()
    _d = {'L0_attn_x': _L0_attn_in['x'], 'L0_attn_w_in': _L0_attn_in['w_in'], 'L0_attn_b_in': _L0_attn_in['b_in'], 'L0_attn_w_a': _L0_attn_in['w_a'], 'L0_attn_b_a': _L0_attn_in['b_a'], 'L0_attn_a_param': _L0_attn_in['a_param'], 'L0_ffn_Wr': _L0_ffn_in['Wr'], 'L0_ffn_W1': _L0_ffn_in['W1'], 'L0_ffn_b1': _L0_ffn_in['b1'], 'L0_ffn_W2': _L0_ffn_in['W2'], 'L0_ffn_b2': _L0_ffn_in['b2'], 'L1_attn_Wqkv': _L1_attn_in['Wqkv'], 'L1_attn_bqkv': _L1_attn_in['bqkv'], 'L1_attn_Wproj': _L1_attn_in['Wproj'], 'L1_attn_bproj': _L1_attn_in['bproj'], 'L1_attn_w1': _L1_attn_in['w1'], 'L1_attn_b1': _L1_attn_in['b1'], 'L1_attn_w2': _L1_attn_in['w2'], 'L1_attn_b2': _L1_attn_in['b2'], 'L1_attn_c_param': _L1_attn_in['c_param'], 'L1_attn_L_multiplier': _L1_attn_in['L_multiplier'], 'L1_ffn_Wqkv': _L1_ffn_in['Wqkv'], 'L1_ffn_q_scale': _L1_ffn_in['q_scale'], 'L1_ffn_k_scale': _L1_ffn_in['k_scale'], 'L1_ffn_Wo': _L1_ffn_in['Wo'], 'L1_ffn_ln_g': _L1_ffn_in['ln_g'], 'L1_ffn_ln_b': _L1_ffn_in['ln_b'], 'L1_ffn_W1': _L1_ffn_in['W1'], 'L1_ffn_b1': _L1_ffn_in['b1'], 'L1_ffn_W2': _L1_ffn_in['W2'], 'L1_ffn_b2': _L1_ffn_in['b2']}
    _x0 = _d['L0_attn_x']
    _d['L0_attn_x'] = jax.random.normal(jax.random.fold_in(jax.random.key(seed), 1), (8, 256, 128), dtype=_x0.dtype)
    del _x0
    return _d

def reference(L0_attn_x, L0_attn_w_in, L0_attn_b_in, L0_attn_w_a, L0_attn_b_a, L0_attn_a_param, L0_ffn_Wr, L0_ffn_W1, L0_ffn_b1, L0_ffn_W2, L0_ffn_b2, L1_attn_Wqkv, L1_attn_bqkv, L1_attn_Wproj, L1_attn_bproj, L1_attn_w1, L1_attn_b1, L1_attn_w2, L1_attn_b2, L1_attn_c_param, L1_attn_L_multiplier, L1_ffn_Wqkv, L1_ffn_q_scale, L1_ffn_k_scale, L1_ffn_Wo, L1_ffn_ln_g, L1_ffn_ln_b, L1_ffn_W1, L1_ffn_b1, L1_ffn_W2, L1_ffn_b2):

    def _L0_attn_ref(x, w_in, b_in, w_a, b_a, a_param):
        import jax, jax.numpy as jnp
        import numpy as np
        B, T, W, H = (8, 512, 128, 8)
        BW = W // H

        def _bdl(x, w, b):
            xh = x.reshape(x.shape[:-1] + (H, BW))
            y = jnp.einsum('bthi,hij->bthj', xh, w) + b
            return y.reshape(x.shape)
        gate_x = jax.nn.sigmoid(_bdl(x, w_in, b_in))
        gate_a = jax.nn.sigmoid(_bdl(x, w_a, b_a))
        log_a = -8.0 * gate_a * jax.nn.softplus(a_param)
        a = jnp.exp(log_a)
        mult = jnp.sqrt(1.0 - jnp.exp(2.0 * log_a))
        reset = (jnp.arange(x.shape[1]) == 0)[None, :, None]
        norm_x = x * gate_x * jnp.where(reset, 1.0, mult)
        a = jnp.where(reset, 0.0, a)

        def comb(c1, c2):
            a1, h1 = c1
            a2, h2 = c2
            return (a1 * a2, a2 * h1 + h2)
        _, y = jax.lax.associative_scan(comb, (a, norm_x), axis=1)
        return y

    def _L0_ffn_ref(x, Wr, W1, b1, W2, b2):
        import jax, jax.numpy as jnp
        import numpy as np
        HIDDEN = 128
        FFN = 512
        N_EXPERTS = 8
        TOP_K = 2
        B, S, D = x.shape
        E = Wr.shape[0]
        xf = x.reshape(-1, D)
        T = xf.shape[0]
        logits = xf @ Wr.T
        probs = jax.nn.softmax(logits, axis=-1)
        top_v, top_i = jax.lax.top_k(probs, TOP_K)
        top_v = top_v / jnp.sum(top_v, axis=-1, keepdims=True)
        comb = jnp.zeros((T, E), dtype=xf.dtype).at[jnp.arange(T)[:, None], top_i].add(top_v)
        h = jax.nn.gelu(jnp.einsum('td,efd->etf', xf, W1) + b1[:, None, :], approximate=False)
        y = jnp.einsum('etf,edf->etd', h, W2) + b2[:, None, :]
        out = jnp.einsum('etd,te->td', y, comb)
        return out.reshape(B, S, D)

    def _L1_attn_ref(x, Wqkv, bqkv, Wproj, bproj, w1, b1, w2, b2, c_param, L_multiplier):
        import jax, jax.numpy as jnp
        import numpy as np
        INIT_L = 512.0
        EPS = 1e-06
        N_HEAD = 16

        def fire_bias(T, w1, b1, w2, b2, c, L_multiplier):
            pos = jnp.arange(T, dtype=jnp.float32)
            rel = pos[:, None] - pos[None, :]
            threshold = jnp.abs(L_multiplier * INIT_L)
            pos_norm = jnp.maximum(pos, threshold)[:, None]
            rel = jnp.log(jnp.abs(c * rel) + 1.0)
            pos_norm = jnp.log(jnp.abs(c * pos_norm) + 1.0) + EPS
            nd = rel / pos_norm
            h = jax.nn.relu(nd[..., None] * w1[0] + b1)
            bias = jnp.einsum('tsw,wh->hts', h, w2) + b2[:, None, None]
            causal = jnp.tril(jnp.ones((T, T), dtype=bool))
            bias = jnp.where(causal[None], bias, -jnp.inf)
            return bias[None]
        B, T, C = x.shape
        H = N_HEAD
        hd = C // H
        qkv = x @ Wqkv + bqkv
        q, k, v = jnp.split(qkv, 3, axis=-1)
        q = q.reshape(B, T, H, hd).transpose(0, 2, 1, 3)
        k = k.reshape(B, T, H, hd).transpose(0, 2, 1, 3)
        v = v.reshape(B, T, H, hd).transpose(0, 2, 1, 3)
        bias = fire_bias(T, w1, b1, w2, b2, c_param, L_multiplier)
        scale = 1.0 / jnp.sqrt(jnp.float32(hd))
        att = jnp.einsum('bhqd,bhkd->bhqk', q, k) * scale + bias
        att = jax.nn.softmax(att, axis=-1)
        y = jnp.einsum('bhqk,bhkd->bhqd', att, v)
        y = y.transpose(0, 2, 1, 3).reshape(B, T, C)
        return y @ Wproj + bproj

    def _L1_ffn_ref(x, Wqkv, q_scale, k_scale, Wo, ln_g, ln_b, W1, b1, W2, b2):
        import jax, jax.numpy as jnp
        import numpy as np
        DIM = 128
        DEPTH = 6
        HEADS = 16
        DIM_HEAD = 64
        WINDOW = 32
        INNER = HEADS * DIM_HEAD
        DIM_INNER = int(DIM * 4 * 2 / 3)
        QK_SCALE = 8.0

        def shift_tokens(t):
            a, s = jnp.split(t, 2, -1)
            s = jnp.pad(s, ((0, 0), (1, 0), (0, 0)))[:, :-1]
            return jnp.concatenate([a, s], -1)

        def l2norm(t):
            return t / jnp.maximum(jnp.linalg.norm(t, axis=-1, keepdims=True), 1e-12)

        def rotate_half(x):
            x1, x2 = jnp.split(x, 2, -1)
            return jnp.concatenate([-x2, x1], -1)

        def rotary_tables(n):
            half = jnp.arange(0, DIM_HEAD, 2, dtype=jnp.float32)
            inv_freq = 1.0 / 10000.0 ** (half / DIM_HEAD)
            t = jnp.arange(n, dtype=jnp.float32)
            freqs = t[:, None] * inv_freq[None, :]
            freqs = jnp.concatenate([freqs, freqs], -1)
            base_scale = (half + 0.4 * DIM_HEAD) / (1.4 * DIM_HEAD)
            power = (t - n // 2) / (WINDOW // 2)
            scale = base_scale[None, :] ** power[:, None]
            scale = jnp.concatenate([scale, scale], -1)
            return (freqs, scale)

        def local_attention(q, k, v):
            b, h, n, d = q.shape
            w = WINDOW
            nw = n // w
            bq = q.reshape(b, h, nw, w, d)
            bk = k.reshape(b, h, nw, w, d)
            bv = v.reshape(b, h, nw, w, d)

            def look(t):
                p = jnp.pad(t, ((0, 0), (0, 0), (1, 0), (0, 0), (0, 0)))
                return jnp.concatenate([p[:, :, :nw], p[:, :, 1:]], axis=3)
            bk2, bv2 = (look(bk), look(bv))
            seq = jnp.arange(n).reshape(nw, w)
            seq_p = jnp.pad(seq, ((1, 0), (0, 0)), constant_values=-1)
            jt = jnp.concatenate([seq_p[:nw], seq_p[1:]], axis=1)
            it = seq[:, :, None]
            jb = jt[:, None, :]
            mask = (it < jb) | (it > jb + w) | (jb == -1)
            sim = jnp.einsum('bhwie,bhwje->bhwij', bq, bk2) * QK_SCALE
            sim = jnp.where(mask, -jnp.finfo(sim.dtype).max, sim)
            attn = jax.nn.softmax(sim, -1)
            out = jnp.einsum('bhwij,bhwje->bhwie', attn, bv2)
            return out.reshape(b, h, n, d)

        def attn_layer(x, Wqkv, qs, ksc, Wo):
            b, n, _ = x.shape
            qkv = x @ Wqkv
            q, k, v = jnp.split(qkv, 3, -1)
            sh = lambda t: t.reshape(b, n, HEADS, DIM_HEAD).transpose(0, 2, 1, 3)
            q, k, v = (sh(q), sh(k), sh(v))
            q = l2norm(q) * qs
            k = l2norm(k) * ksc
            freqs, scale = rotary_tables(n)
            cos, sin = (jnp.cos(freqs), jnp.sin(freqs))
            q = q * cos * scale + rotate_half(q) * sin * scale
            inv = 1.0 / scale
            k = k * cos * inv + rotate_half(k) * sin * inv
            out = local_attention(q, k, v)
            out = out.transpose(0, 2, 1, 3).reshape(b, n, INNER)
            return out @ Wo

        def ffn_layer(x, g, bln, W1, b1, W2, b2):
            mu = x.mean(-1, keepdims=True)
            var = ((x - mu) ** 2).mean(-1, keepdims=True)
            xn = (x - mu) / jnp.sqrt(var + 1e-05) * g + bln
            hg = xn @ W1 + b1
            a, gate = jnp.split(hg, 2, -1)
            return a * jax.nn.gelu(gate, approximate=False) @ W2 + b2
        for i in range(DEPTH):
            x = attn_layer(shift_tokens(x), Wqkv[i], q_scale[i], k_scale[i], Wo[i]) + x
            x = ffn_layer(shift_tokens(x), ln_g[i], ln_b[i], W1[i], b1[i], W2[i], b2[i]) + x
        return x
    x = L0_attn_x
    x = x + 0.5 * _L0_ffn_ref(_layernorm(x, axis=-1), L0_ffn_Wr, L0_ffn_W1, L0_ffn_b1, L0_ffn_W2, L0_ffn_b2)
    x = x + _L0_attn_ref(_layernorm(x, axis=-1), L0_attn_w_in, L0_attn_b_in, L0_attn_w_a, L0_attn_b_a, L0_attn_a_param)
    x = x + 0.5 * _L0_ffn_ref(_layernorm(x, axis=-1), L0_ffn_Wr, L0_ffn_W1, L0_ffn_b1, L0_ffn_W2, L0_ffn_b2)
    x = x + 0.5 * _L1_ffn_ref(_layernorm(x, axis=-1), L1_ffn_Wqkv, L1_ffn_q_scale, L1_ffn_k_scale, L1_ffn_Wo, L1_ffn_ln_g, L1_ffn_ln_b, L1_ffn_W1, L1_ffn_b1, L1_ffn_W2, L1_ffn_b2)
    x = x + _L1_attn_ref(_layernorm(x, axis=-1), L1_attn_Wqkv, L1_attn_bqkv, L1_attn_Wproj, L1_attn_bproj, L1_attn_w1, L1_attn_b1, L1_attn_w2, L1_attn_b2, L1_attn_c_param, L1_attn_L_multiplier)
    x = x + 0.5 * _L1_ffn_ref(_layernorm(x, axis=-1), L1_ffn_Wqkv, L1_ffn_q_scale, L1_ffn_k_scale, L1_ffn_Wo, L1_ffn_ln_g, L1_ffn_ln_b, L1_ffn_W1, L1_ffn_b1, L1_ffn_W2, L1_ffn_b2)
    return x

_drawn_inputs = setup_inputs


def setup_inputs(seed=0):
    import zlib

    import numpy as np

    out = dict(_drawn_inputs(seed))
    spreads = {'L0_attn_b_in': (0.0, 0.506),
     'L0_attn_b_a': (0.0, 0.703),
     'L0_ffn_b1': (0.0, 0.439),
     'L0_ffn_b2': (0.0, 0.1),
     'L1_attn_bqkv': (0.0, 0.644),
     'L1_attn_bproj': (0.0, 0.369),
     'L1_attn_b1': (0.0, 2.0),
     'L1_attn_b2': (0.0, 2.0),
     'L1_ffn_q_scale': (1.0, 0.6),
     'L1_ffn_k_scale': (1.0, 0.6),
     'L1_ffn_ln_g': (1.0, 0.6),
     'L1_ffn_ln_b': (0.0, 0.8),
     'L1_ffn_b1': (0.0, 0.8),
     'L1_ffn_b2': (0.0, 0.1)}
    factors = {'L1_attn_Wqkv': 7.138,
     'L1_attn_Wproj': 3.799,
     'L1_attn_w1': 8.0,
     'L1_attn_w2': 8.0,
     'L1_ffn_W1': 3.806,
     'L1_ffn_W2': 3.735}
    for name, (base, spread) in spreads.items():
        noise = np.random.default_rng([zlib.crc32(name.encode()), seed]).standard_normal(out[name].shape)
        drawn = base * np.exp(spread * noise) if base else spread * noise
        out[name] = jnp.asarray(drawn.astype(out[name].dtype))
    for name, factor in factors.items():
        out[name] = (out[name] * factor).astype(out[name].dtype)
    return out
```

```python
import numpy as np
import concourse.bass as bass
from concourse import mybir
from contextlib import ExitStack

FP32 = mybir.dt.float32
BF16 = mybir.dt.bfloat16
ALU = mybir.AluOpType
ACT = mybir.ActivationFunctionType
AX = mybir.AxisListType

P = 128
B, T = 8, 256
NT = B * T
CH = 512
NC = NT // CH
TILES = NT // P
BIG = 1.0e30
EPS = 1e-5

EXPERTS, FFN = 8, 512
FB = FFN // P
RH, RW = 8, 16
NH, HD, BW = 16, 8, 32
INIT_L = 512.0
DEPTH, HEADS, DH, WIN = 6, 16, 64, 32
INNER = HEADS * DH
DI = int(P * 4 * 2 / 3)
HG = 4
GJ = HEADS // HG
GB = 2 * GJ
XS = T + 1
DB = [(0, 128), (128, 128), (256, DI - 256)]
GROUPCOLS = 3 * HG * DH


def layer_norm_block(nc, res, src, dst, add_shifted=None):
    bank, avg, eps = res["bank"], res["avg"], res["eps"]
    with ExitStack() as ctx:
        phase = res["phase"] = res["phase"] + 1

        def sb(name, shape, dt=FP32):
            return ctx.enter_context(nc.sbuf_tensor(f"{name}_{phase}", shape, dt))

        def sem(name):
            s = ctx.enter_context(nc.semaphore(f"{name}_{phase}"))
            sems.append(s)
            return s
        sems = []
        dev = sb("ln_dev", [P, NT])
        sq = sb("ln_sq", [P, NT])
        rstd = sb("ln_rstd", [P, NT])
        added, mean_done, dev_done, sq_done = sem("ln_added"), sem("ln_mean"), sem("ln_devs"), sem("ln_sqs")
        var_done, log_done, rstd_done = sem("ln_var"), sem("ln_log"), sem("ln_rstds")

        with nc.Block() as block:
            @block.tensor
            def _(pe):
                for c in range(NC):
                    if add_shifted is not None:
                        pe.wait_ge(added, 4 * (c + 1))
                    nc.tensor.matmul(bank[c][:, :], avg[:, :], src[:, c * CH:(c + 1) * CH],
                                     start=True, stop=True).then_inc(mean_done, 1)
                for c in range(NC):
                    pe.wait_ge(sq_done, c + 1)
                    nc.tensor.matmul(bank[4 + c][:, :], avg[:, :], sq[:, c * CH:(c + 1) * CH],
                                     start=True, stop=True).then_inc(var_done, 1)

            @block.vector
            def _(dve):
                if add_shifted is not None:
                    for b in range(B):
                        for lo, sh in ((0, 0), (64, 1)):
                            m = src[lo:lo + 64, b * T:(b + 1) * T]
                            x = add_shifted[lo:lo + 64, b * XS + sh:b * XS + sh + T]
                            nc.vector.scalar_tensor_tensor(out=m, in0=x, scalar=0.5, in1=m,
                                                           op0=ALU.mult, op1=ALU.add).then_inc(added, 1)
                for c in range(NC):
                    s = slice(c * CH, (c + 1) * CH)
                    dve.wait_ge(mean_done, c + 1)
                    nc.vector.tensor_tensor(dev[:, s], src[:, s], bank[c][:, :], ALU.subtract).then_inc(dev_done, 1)
                for c in range(NC):
                    dve.wait_ge(rstd_done, c + 1)
                    for o, i in dst(c):
                        nc.vector.tensor_tensor(o, i(dev), i(rstd), ALU.mult)

            @block.scalar
            def _(act):
                for c in range(NC):
                    s = slice(c * CH, (c + 1) * CH)
                    act.wait_ge(dev_done, c + 1)
                    nc.scalar.activation(sq[:, s], dev[:, s], ACT.Square).then_inc(sq_done, 1)
                for c in range(NC):
                    s = slice(c * CH, (c + 1) * CH)
                    act.wait_ge(var_done, c + 1)
                    nc.scalar.activation(rstd[:, s], bank[4 + c][:, :], ACT.Ln, bias=eps[:, 0:1]).then_inc(log_done, 1)
                for c in range(NC):
                    s = slice(c * CH, (c + 1) * CH)
                    act.wait_ge(log_done, c + 1)
                    nc.scalar.activation(rstd[:, s], rstd[:, s], ACT.Exp, scale=-0.5).then_inc(rstd_done, 1)
        clear(nc, sems)


def clear(nc, sems):
    with nc.Block() as block:
        @block.gpsimd
        def _(pool):
            for s in sems:
                pool.sem_clear(s)


def plain(dst):
    def pieces(c):
        s = slice(c * CH, (c + 1) * CH)
        return [(dst[:, s], lambda t: t[:, s])]
    return pieces


def shifted(dst):
    def pieces(c):
        out = []
        for b in (2 * c, 2 * c + 1):
            for lo, sh in ((0, 0), (64, 1)):
                out.append((dst[lo:lo + 64, b * XS + sh:b * XS + sh + T],
                            lambda t, lo=lo, b=b: t[lo:lo + 64, b * T:(b + 1) * T]))
        return out
    return pieces


def moe_phase(nc, res, d, M, XN):
    bank, ident = res["bank"], res["ident"]
    with ExitStack() as ctx:
        phase = res["phase"] = res["phase"] + 1

        def sb(name, shape, dt=FP32):
            return ctx.enter_context(nc.sbuf_tensor(f"{name}_{phase}", shape, dt))

        def sem(name):
            s = ctx.enter_context(nc.semaphore(f"{name}_{phase}"))
            sems.append(s)
            return s
        sems = []
        w1 = sb("moe_w1", [P, 2, FFN])
        w2 = sb("moe_w2", [P, 2, FFN])
        bb = sb("moe_bb", [P, 2, FB + 1])
        wr = sb("moe_wr", [P, EXPERTS])
        lg = sb("moe_lg", [P, TILES, EXPERTS])
        pr = sb("moe_pr", [P, TILES, EXPERTS])
        eq = sb("moe_eq", [P, TILES, EXPERTS])
        one1 = sb("moe_one1", [P, TILES, EXPERTS])
        comb = sb("moe_comb", [P, TILES, EXPERTS])
        m1 = sb("moe_m1", [P, TILES])
        m2 = sb("moe_m2", [P, TILES])
        den = sb("moe_den", [P, TILES])
        combT = sb("moe_combT", [EXPERTS, NT])
        cbc = sb("moe_cbc", [P, 2, NT])
        H = sb("moe_H", [P, 2, FB * CH])
        tmp = sb("moe_tmp", [P, 2, CH])
        ldr, lgd, dch = sem("moe_ldr"), sem("moe_lgd"), sem("moe_dch")
        combd, combT_d, combT_e = sem("moe_combd"), sem("moe_combTd"), sem("moe_combTe")
        stored, cb_ld = sem("moe_stored"), [sem("moe_cbld0"), sem("moe_cbld1")]
        w_ld = [sem("moe_wld0"), sem("moe_wld1")]
        up, act_d, down, weighed, added = sem("moe_up"), sem("moe_act"), sem("moe_down"), sem("moe_weighed"), sem("moe_added")
        rank = res["rank"]
        TE = TILES * EXPERTS

        def bc(ap):
            return ap.unsqueeze(2).to_broadcast([P, TILES, EXPERTS])

        with nc.Block() as block:
            @block.sync
            def _(sp):
                sp.dma_start(wr[:, :], d["moe_wr"]).then_inc(ldr, 16)
                sp.wait_ge(combT_e, TILES // 4)
                sp.dma_start(d["comb_scratch"], combT[:, :]).then_inc(stored, 16)
                sp.wait_ge(stored, 16)

            @block.tensor
            def _(pe):
                pe.wait_ge(ldr, 16)
                for t in range(TILES):
                    nc.tensor.matmul(bank[0][:, t * EXPERTS:(t + 1) * EXPERTS], XN[:, t * P:(t + 1) * P],
                                     wr[:, :], start=True, stop=True).then_inc(lgd, 1)
                pe.wait_ge(combd, 1)
                for q in range(TILES // 4):
                    for t in range(4 * q, 4 * q + 4):
                        last = nc.tensor.transpose(bank[1 + q][0:EXPERTS, (t % 4) * P:(t % 4 + 1) * P],
                                                   comb[:, t, :], ident[:, :])
                    last.then_inc(combT_d, 1)

            @block.scalar
            def _(act):
                act.wait_ge(dch, 2)
                nc.scalar.activation(pr[:, :, :], lg[:, :, :], ACT.Exp).then_inc(lgd, 1)
                for q in range(TILES // 4):
                    act.wait_ge(combT_d, q + 1)
                    nc.scalar.activation(combT[:, q * CH:(q + 1) * CH], bank[1 + q][0:EXPERTS, :],
                                         ACT.Copy).then_inc(combT_e, 1)

            @block.vector
            def _(dve):
                n = [0]

                def link(ins):
                    n[0] += 1
                    ins.then_inc(dch, 1)
                    dve.wait_ge(dch, n[0])
                L = bank[0][:, 0:TE].rearrange("p (t e) -> p t e", e=EXPERTS)
                dve.wait_ge(lgd, TILES)
                link(nc.vector.tensor_reduce(m1[:, :], L, AX.X, ALU.max))
                link(nc.vector.tensor_tensor(lg[:, :, :], L, bc(m1[:, :]), ALU.subtract))
                dve.wait_ge(lgd, TILES + 1)
                link(nc.vector.tensor_reduce(den[:, :], pr[:, :, :], AX.X, ALU.add))
                link(nc.vector.reciprocal(den[:, :], den[:, :]))
                link(nc.vector.tensor_tensor(pr[:, :, :], pr[:, :, :], bc(den[:, :]), ALU.mult))
                link(nc.vector.tensor_reduce(m1[:, :], pr[:, :, :], AX.X, ALU.max))
                link(nc.vector.tensor_tensor(eq[:, :, :], pr[:, :, :], bc(m1[:, :]), ALU.is_equal))
                link(nc.vector.tensor_tensor(eq[:, :, :], eq[:, :, :], rank[:, :, :], ALU.mult))
                link(nc.vector.tensor_reduce(den[:, :], eq[:, :, :], AX.X, ALU.max))
                link(nc.vector.tensor_tensor(one1[:, :, :], eq[:, :, :], bc(den[:, :]), ALU.is_equal))
                link(nc.vector.scalar_tensor_tensor(out=lg[:, :, :], in0=one1[:, :, :], scalar=-2.0,
                                                    in1=pr[:, :, :], op0=ALU.mult, op1=ALU.add))
                link(nc.vector.tensor_reduce(m2[:, :], lg[:, :, :], AX.X, ALU.max))
                link(nc.vector.tensor_tensor(eq[:, :, :], lg[:, :, :], bc(m2[:, :]), ALU.is_equal))
                link(nc.vector.tensor_tensor(eq[:, :, :], eq[:, :, :], rank[:, :, :], ALU.mult))
                link(nc.vector.tensor_reduce(den[:, :], eq[:, :, :], AX.X, ALU.max))
                link(nc.vector.tensor_tensor(eq[:, :, :], eq[:, :, :], bc(den[:, :]), ALU.is_equal))
                link(nc.vector.tensor_tensor(den[:, :], m1[:, :], m2[:, :], ALU.add))
                link(nc.vector.reciprocal(den[:, :], den[:, :]))
                link(nc.vector.tensor_scalar(den[:, :], den[:, :], 0.5, None, ALU.mult))
                link(nc.vector.tensor_tensor(m1[:, :], m1[:, :], den[:, :], ALU.mult))
                link(nc.vector.tensor_tensor(m2[:, :], m2[:, :], den[:, :], ALU.mult))
                link(nc.vector.tensor_tensor(one1[:, :, :], one1[:, :, :], bc(m1[:, :]), ALU.mult))
                link(nc.vector.tensor_tensor(eq[:, :, :], eq[:, :, :], bc(m2[:, :]), ALU.mult))
                nc.vector.tensor_tensor(comb[:, :, :], one1[:, :, :], eq[:, :, :], ALU.add).then_inc(combd, 1)

        def idx(e, c):
            return e * NC + c

        with nc.Block() as block:
            @block.sync
            def _(sp):
                def load(e, par):
                    for w, name in ((w1, "moe_w1"), (w2, "moe_w2"), (bb, "moe_bb")):
                        sp.dma_start(w[:, par, :], d[name][bass.ds(e, 1), :, :].rearrange("a p n -> (a p) n"))\
                          .then_inc(w_ld[par], 16)
                    sp.dma_start(cbc[:, par, :],
                                 d["comb_scratch"][bass.ds(e, 1), :].to_broadcast([P, NT])).then_inc(cb_ld[par], 16)
                load(0, 0)
                load(1, 1)
                with sp.Fori(1, EXPERTS // 2) as k:
                    for par in range(2):
                        sp.wait_ge(weighed, k * (2 * NC) + (par * NC - NC))
                        load(k * 2 + par, par)

            @block.tensor
            def _(pe):
                def hidden(e, par, c, first):
                    if c == 0:
                        pe.wait_ge(w_ld[par], (e - par) * 24 + 48)
                    for f in range(FB):
                        if not (first and c * FB + f < 4 and par == 0):
                            pe.wait_ge(act_d, idx(e, c) * FB + (f - 3))
                        nc.tensor.matmul(bank[f][:, :], w1[:, par, f * P:(f + 1) * P],
                                         XN[:, c * CH:(c + 1) * CH], start=True, stop=True).then_inc(up, 1)

                def out(e, par, c, first):
                    if not (first and c < 2 and par == 0):
                        pe.wait_ge(weighed, idx(e, c) - 1)
                    for f in range(FB):
                        pe.wait_ge(act_d, idx(e, c) * FB + (f + 1))
                        i = nc.tensor.matmul(bank[4 + c % 2][:, :], w2[:, par, f * P:(f + 1) * P],
                                             H[:, c % 2, f * CH:(f + 1) * CH], start=(f == 0), stop=(f == FB - 1))
                    i.then_inc(down, 1)

                def pair(k, first):
                    for par in range(2):
                        for c in range(NC):
                            hidden(k * 2 + par, par, c, first)
                            if c:
                                out(k * 2 + par, par, c - 1, first)
                            elif par or not first:
                                e_before = k * 2 + (par - 1)
                                out(e_before, 1 - par, NC - 1, False)
                pair(0, True)
                with pe.Fori(1, EXPERTS // 2) as k:
                    pair(k, False)
                out(EXPERTS - 1, 1, NC - 1, False)

            @block.scalar
            def _(act):
                def gelus(e, par, c, first):
                    if not (first and c < 2 and par == 0):
                        act.wait_ge(down, idx(e, c) - 1)
                    if c == 0:
                        act.wait_ge(w_ld[par], (e - par) * 24 + 48)
                    for f in range(FB):
                        act.wait_ge(up, idx(e, c) * FB + (f + 1))
                        nc.scalar.activation(H[:, c % 2, f * CH:(f + 1) * CH], bank[f][:, :], ACT.Gelu,
                                             bias=bb[:, par, f:f + 1]).then_inc(act_d, 1)

                def pair(k, first):
                    for par in range(2):
                        for c in range(NC):
                            gelus(k * 2 + par, par, c, first)
                pair(0, True)
                with act.Fori(1, EXPERTS // 2) as k:
                    pair(k, False)

            @block.vector
            def _(dve):
                def weigh(k, par, c, first):
                    e = k * 2 + par
                    if c == 0:
                        dve.wait_ge(cb_ld[par], k * 16 + 16)
                        dve.wait_ge(w_ld[par], k * 48 + 48)
                    dve.wait_ge(down, idx(e, c) + 1)
                    if not (first and par == 0 and c < 2):
                        dve.wait_ge(added, idx(e, c) - 1)
                    nc.vector.scalar_tensor_tensor(out=tmp[:, c % 2, :], in0=bank[4 + c % 2][:, :],
                                                   scalar=bb[:, par, FB:FB + 1], in1=cbc[:, par, c * CH:(c + 1) * CH],
                                                   op0=ALU.add, op1=ALU.mult).then_inc(weighed, 1)
                for par in range(2):
                    for c in range(NC):
                        weigh(0, par, c, True)
                with dve.Fori(1, EXPERTS // 2) as k:
                    for par in range(2):
                        for c in range(NC):
                            weigh(k, par, c, False)

            @block.gpsimd
            def _(pool):
                def add(e, par, c, first):
                    pool.wait_ge(weighed, idx(e, c) + 1)
                    if not (first and par == 0):
                        pool.wait_ge(added, idx(e, c) - (NC - 1))
                    m = M[:, c * CH:(c + 1) * CH]
                    nc.gpsimd.tensor_tensor(m, m, tmp[:, c % 2, :], ALU.add).then_inc(added, 1)
                for par in range(2):
                    for c in range(NC):
                        add(par, par, c, True)
                with pool.Fori(1, EXPERTS // 2) as k:
                    for par in range(2):
                        for c in range(NC):
                            add(k * 2 + par, par, c, False)
        clear(nc, sems)


def recurrence_phase(nc, res, d, M, XN):
    bank = res["bank"]
    with ExitStack() as ctx:
        phase = res["phase"] = res["phase"] + 1

        def sb(name, shape, dt=FP32):
            return ctx.enter_context(nc.sbuf_tensor(f"{name}_{phase}", shape, dt))

        def sem(name):
            s = ctx.enter_context(nc.semaphore(f"{name}_{phase}"))
            sems.append(s)
            return s
        sems = []
        win, wa = sb("rg_win", [P, P]), sb("rg_wa", [P, P])
        vec = sb("rg_vec", [P, 3])
        v = sb("rg_v", [P, 8])
        gx, ga, th = sb("rg_gx", [P, NT]), sb("rg_ga", [P, NT]), sb("rg_th", [P, NT])
        den, a, h = sb("rg_den", [P, NT]), sb("rg_a", [P, NT]), sb("rg_h", [P, NT])
        zero_d, ld, vch, gates = sem("rg_zero"), sem("rg_ld"), sem("rg_vch"), sem("rg_gates")
        gx_d, ga_d, th_d, a_d, den_d = sem("rg_gxd"), sem("rg_gad"), sem("rg_thd"), sem("rg_ad"), sem("rg_dend")
        ratio_d, mult_d, nx_d, fix_d = sem("rg_ratio"), sem("rg_mult"), sem("rg_nx"), sem("rg_fix")
        softch, scan_d = sem("rg_soft"), sem("rg_scan")

        with nc.Block() as block:
            @block.gpsimd
            def _(pool):
                nc.gpsimd.memset(win[:, :], 0.0).then_inc(zero_d, 1)
                nc.gpsimd.memset(wa[:, :], 0.0).then_inc(zero_d, 1)

            @block.sync
            def _(sp):
                sp.dma_start(vec[:, :], d["rg_vec"]).then_inc(ld, 16)
                sp.wait_ge(zero_d, 2)
                for w, name in ((win, "rg_win"), (wa, "rg_wa")):
                    for r in range(RH):
                        s = slice(r * RW, (r + 1) * RW)
                        sp.dma_start(w[s, s], d[name][r, :, :]).then_inc(ld, 16)

            @block.tensor
            def _(pe):
                pe.wait_ge(ld, 16 * (1 + 2 * RH))
                for c in range(NC):
                    s = slice(c * CH, (c + 1) * CH)
                    nc.tensor.matmul(bank[c][:, :], win[:, :], XN[:, s], start=True, stop=True).then_inc(gates, 1)
                    nc.tensor.matmul(bank[4 + c][:, :], wa[:, :], XN[:, s], start=True, stop=True).then_inc(gates, 1)

            @block.scalar
            def _(act):
                act.wait_ge(ld, 16 * (1 + 2 * RH))
                nc.scalar.activation(v[:, 0:1], vec[:, 2:3], ACT.Abs).then_inc(softch, 1)
                act.wait_ge(softch, 1)
                nc.scalar.activation(v[:, 1:2], v[:, 0:1], ACT.Exp, scale=-1.0).then_inc(softch, 1)
                act.wait_ge(vch, 1)
                nc.scalar.activation(v[:, 3:4], v[:, 2:3], ACT.Ln).then_inc(softch, 1)
                for c in range(NC):
                    s = slice(c * CH, (c + 1) * CH)
                    act.wait_ge(gates, 2 * (c + 1))
                    nc.scalar.activation(gx[:, s], bank[c][:, :], ACT.Sigmoid, bias=vec[:, 0:1]).then_inc(gx_d, 1)
                    nc.scalar.activation(ga[:, s], bank[4 + c][:, :], ACT.Sigmoid, bias=vec[:, 1:2]).then_inc(ga_d, 1)
                act.wait_ge(vch, 9)
                for c in range(NC):
                    s = slice(c * CH, (c + 1) * CH)
                    act.wait_ge(ga_d, c + 1)
                    nc.scalar.activation(th[:, s], ga[:, s], ACT.Tanh, scale=v[:, 6:7]).then_inc(th_d, 1)
                for c in range(NC):
                    s = slice(c * CH, (c + 1) * CH)
                    nc.scalar.activation(a[:, s], ga[:, s], ACT.Exp, scale=v[:, 7:8]).then_inc(a_d, 1)
                for c in range(NC):
                    s = slice(c * CH, (c + 1) * CH)
                    act.wait_ge(ratio_d, c + 1)
                    nc.scalar.activation(th[:, s], th[:, s], ACT.Sqrt, scale=2.0).then_inc(mult_d, 1)

            @block.vector
            def _(dve):
                n = [0]

                def link(ins):
                    n[0] += 1
                    ins.then_inc(vch, 1)
                    dve.wait_ge(vch, n[0])
                dve.wait_ge(softch, 2)
                link(nc.vector.tensor_scalar(v[:, 2:3], v[:, 1:2], 1.0, None, ALU.add))
                link(nc.vector.tensor_scalar(v[:, 4:5], v[:, 2:3], 1.0, 1e-30, ALU.subtract, ALU.max))
                link(nc.vector.reciprocal(v[:, 5:6], v[:, 4:5]))
                link(nc.vector.tensor_tensor(v[:, 5:6], v[:, 5:6], v[:, 1:2], ALU.mult))
                dve.wait_ge(softch, 3)
                link(nc.vector.tensor_tensor(v[:, 5:6], v[:, 5:6], v[:, 3:4], ALU.mult))
                link(nc.vector.scalar_tensor_tensor(out=v[:, 6:7], in0=v[:, 4:5], scalar=1e-20, in1=v[:, 1:2],
                                                    op0=ALU.is_lt, op1=ALU.mult))
                link(nc.vector.scalar_tensor_tensor(out=v[:, 5:6], in0=vec[:, 2:3], scalar=0.0, in1=v[:, 5:6],
                                                    op0=ALU.max, op1=ALU.add))
                link(nc.vector.tensor_tensor(v[:, 5:6], v[:, 5:6], v[:, 6:7], ALU.add))
                nc.vector.tensor_scalar(v[:, 6:7], v[:, 5:6], 8.0, None, ALU.mult)
                link(nc.vector.tensor_scalar(v[:, 7:8], v[:, 5:6], -8.0, None, ALU.mult))
                for c in range(NC):
                    s = slice(c * CH, (c + 1) * CH)
                    dve.wait_ge(gx_d, c + 1)
                    nc.vector.tensor_tensor(gx[:, s], gx[:, s], XN[:, s], ALU.mult).then_inc(nx_d, 1)
                for c in range(NC):
                    s = slice(c * CH, (c + 1) * CH)
                    dve.wait_ge(th_d, c + 1)
                    nc.vector.tensor_scalar(den[:, s], th[:, s], 1.0, None, ALU.add).then_inc(den_d, 1)
                    dve.wait_ge(den_d, 2 * c + 1)
                    nc.vector.reciprocal(den[:, s], den[:, s]).then_inc(den_d, 1)
                    dve.wait_ge(den_d, 2 * c + 2)
                    nc.vector.tensor_tensor(th[:, s], th[:, s], den[:, s], ALU.mult).then_inc(ratio_d, 1)
                dve.wait_ge(a_d, NC)
                dve.wait_ge(mult_d, NC)
                nc.vector.memset(a[:, 0:NT:T], 0.0).then_inc(fix_d, 1)
                nc.vector.memset(th[:, 0:NT:T], 1.0).then_inc(fix_d, 1)
                dve.wait_ge(fix_d, 2)
                dve.wait_ge(nx_d, NC)
                nc.vector.tensor_tensor(gx[:, :], gx[:, :], th[:, :], ALU.mult).then_inc(nx_d, 1)
                dve.wait_ge(nx_d, NC + 1)
                nc.vector.tensor_tensor_scan(h[:, :], a[:, :], gx[:, :], 0.0, ALU.mult, ALU.add).then_inc(scan_d, 1)
                dve.wait_ge(scan_d, 1)
                nc.vector.tensor_tensor(M[:, :], M[:, :], h[:, :], ALU.add)
        clear(nc, sems)


def local_transformer_phase(nc, res, d, X, call):
    bank, avg, eps, ident, identb = res["bank"], res["avg"], res["eps"], res["ident"], res["identb"]
    A, V_, TB, S_, PTB, O_, W_ = bank[0:2], bank[2], bank[3], bank[4], bank[5], bank[6], bank[7]
    with ExitStack() as ctx:
        phase = res["phase"] = res["phase"] + 1

        def sb(name, shape, dt=FP32):
            return ctx.enter_context(nc.sbuf_tensor(f"{name}_{phase}", shape, dt))

        def sem(name, into=None):
            s = ctx.enter_context(nc.semaphore(f"{name}_{phase}"))
            (asems if into is None else into).append(s)
            return s
        asems, fsems, isems = [], [], []
        wqkv = sb("lt_wqkv", [P, 3 * INNER])
        wo = sb("lt_wo", [P, INNER])
        w1 = sb("lt_w1", [P, 2 * DI])
        w2 = sb("lt_w2", [P, 3 * P])
        fv = sb("lt_fv", [P, 9])
        qs = sb("lt_qs", [P, 4 * DH])
        tab = sb("lt_tab", [P, 2, 2, 2, HG, DH])
        xc = sb("lt_xc", [P, 2, P])
        sq = sb("lt_sq", [P, 2, 512])
        t1 = sb("lt_t1", [P, 2, 512])
        t2 = sb("lt_t2", [P, 2, 512])
        qk = sb("lt_qk", [P, 2, 512])
        ss = sb("lt_ss", [P, 2, 8])
        rn = sb("lt_rn", [P, 2, 8])
        qT = sb("lt_qT", [P, 2, 2, P])
        kz = sb("lt_kz", [P, GB, HG, P])
        vv = sb("lt_vv", [P, GB, HG, DH + 1])
        mx = sb("lt_mx", [P, 2, HG])
        pb = sb("lt_pb", [P, 2, HG, P])
        pT = sb("lt_pT", [P, 2, 2, HG, P])
        pprev = sb("lt_pprev", [P, 2, HG, WIN])
        rd = sb("lt_rd", [P, 2, HG])
        on = sb("lt_on", [P, 2, HG, DH])
        oT = sb("lt_oT", [P, 2, 2, P])
        dev, sqf, rs = sb("lt_dev", [P, NT]), sb("lt_sqf", [P, NT]), sb("lt_rs", [P, NT])
        gl = sb("lt_gl", [P, 2, 3, CH])
        hh = sb("lt_hh", [P, 2, 3, CH])
        cst, mainb, prevb, mhalf = res["rot"], res["mainb"], res["prevb"], res["mhalf"]

        def load_attention_weights(sp, s, layer):
            sp.dma_start(wqkv[:, :], d["lt_wqkv"][bass.ds(layer, 1), :, :].rearrange("a p n -> (a p) n")).then_inc(s, 16)
            sp.dma_start(wo[:, :], d["lt_wo"][bass.ds(layer, 1), :, :].rearrange("a p n -> (a p) n")).then_inc(s, 16)
            sp.dma_start(qs[:, :], d["lt_qs"][bass.ds(layer, 1), :].to_broadcast([P, 4 * DH])).then_inc(s, 16)

        def make_tables(pool, s):
            for t in range(2):
                for cs in range(2):
                    for w in range(2):
                        sc = qs[:, (2 * cs + w) * DH:(2 * cs + w + 1) * DH]
                        co = cst[:, ((t * 2 + cs) * 2 + w) * DH:((t * 2 + cs) * 2 + w + 1) * DH]
                        nc.gpsimd.tensor_tensor(tab[:, t, cs, w, :, :], co.unsqueeze(1).to_broadcast([P, HG, DH]),
                                                sc.unsqueeze(1).to_broadcast([P, HG, DH]), ALU.mult).then_inc(s, 1)

        il, iz = sem("lt_il", isems), sem("lt_iz", isems)
        with nc.Block() as block:
            @block.sync
            def _(sp):
                load_attention_weights(sp, il, 0)
                sp.wait_ge(il, 48)

            @block.vector
            def _(dve):
                nc.vector.memset(kz[:, :, :, :], 0.0)
                nc.vector.memset(pT[:, :, :, :, :], 0.0)
                nc.vector.memset(pprev[:, :, :, :], 0.0)
                nc.vector.memset(vv[:, :, :, :], 1.0)

            @block.gpsimd
            def _(pool):
                pool.wait_ge(il, 48)
                make_tables(pool, iz)

        qkp, sqd, rot, ssd, prep, qkd = [sem("lt_" + n) for n in ("qkp", "sqd", "rot", "ssd", "prep", "qkd")]
        tT, tE, simd, mxd, subd, expd = [sem("lt_" + n) for n in ("tT", "tE", "simd", "mxd", "subd", "expd")]
        ptT, ptE, pvd, rdd, ond, oTd = [sem("lt_" + n) for n in ("ptT", "ptE", "pvd", "rdd", "ond", "oTd")]
        oTe, wod, xup, vp, vE, wld = [sem("lt_" + n) for n in ("oTe", "wod", "xup", "vp", "vE", "wld")]
        padd, xcd = sem("lt_padd"), sem("lt_xcd")
        fmean, fdev, fsq, fvar, flog, frs = [sem("lt_f" + n, fsems) for n in ("mean", "dev", "sq", "var", "log", "rs")]
        fn1, fn2, fgp, fgd, fhd, fy = [sem("lt_f" + n, fsems) for n in ("n1", "n2", "gp", "gd", "hd", "y")]
        wnext, ftab, fx = sem("lt_wnext", fsems), sem("lt_ftab", fsems), sem("lt_fx", fsems)

        def grp(g):
            b, i = g
            return b, i, i // GJ, i % GJ, i % 2

        def back(g, k):
            b, i = g
            i -= k
            while i < 0:
                b, i = b - 1, i + GB
            return None if isinstance(b, int) and b < 0 else (b, i)

        def upto(eng, s, g, k=0, per=1):
            q = back(g, k)
            if q is not None:
                eng.wait_ge(s, q[0] * (GB * per) + (q[1] + 1) * per)

        def pipeline(eng, slot, tail):
            for i in range(GB):
                slot((0, i), True)
            with eng.Fori(1, B) as b:
                for i in range(GB):
                    slot((b, i), True)
            for i in range(tail):
                slot((B, i), False)

        with nc.Fori(0, DEPTH) as layer:
            with nc.Block() as block:
                @block.sync
                def _(sp):
                    sp.dma_start(w1[:, :], d["lt_w1"][bass.ds(layer, 1), :, :].rearrange("a p n -> (a p) n")).then_inc(wld, 16)
                    sp.dma_start(w2[:, :], d["lt_w2"][bass.ds(layer, 1), :, :].rearrange("a p n -> (a p) n")).then_inc(wld, 16)
                    sp.dma_start(fv[:, :], d["lt_fv"][bass.ds(layer, 1), :, :].rearrange("a p n -> (a p) n")).then_inc(wld, 16)
                    sp.wait_ge(wld, 48)

                @block.tensor
                def _(pe):
                    def slot(g, live):
                        g2, g3, g4 = back(g, 2), back(g, 3), back(g, 4)
                        b, i, t, j, par = grp(g)
                        if g2 is not None and (live or g2[1] >= GB - 2):
                            _, _, _, _, p2 = grp(g2)
                            upto(pe, qkd, g2)
                            upto(pe, oTe, g2, 3)
                            for q in range(4):
                                ins = nc.tensor.transpose(TB[:, q * P:(q + 1) * P], qk[:, p2, q * P:(q + 1) * P], ident[:, :])
                            ins.then_inc(tT, 1)
                        if live:
                            upto(pe, rot, g, 2)
                            if j == 0:
                                pe.wait_ge(xcd, b * 2 + (t + 1))
                            nc.tensor.matmul(A[par][:, :], xc[:, t, :], wqkv[:, j * GROUPCOLS:j * GROUPCOLS + 512],
                                             start=True, stop=True).then_inc(qkp, 1)
                        if g3 is not None and (live or g3[1] >= GB - 3):
                            _, _, _, _, p3 = grp(g3)
                            upto(pe, expd, g3)
                            upto(pe, ptE, g3, 1)
                            for h in range(HG):
                                ins = nc.tensor.transpose(PTB[:, h * P:(h + 1) * P], pb[:, p3, h, :], ident[:, :])
                            ins.then_inc(ptT, 1)
                        if live:
                            upto(pe, vE, g, 1)
                            nc.tensor.matmul(V_[:, 0:HG * DH], xc[:, t, :], wqkv[:, j * GROUPCOLS + 512:(j + 1) * GROUPCOLS],
                                             start=True, stop=True).then_inc(vp, 1)
                        if g2 is not None and (live or g2[1] >= GB - 2):
                            _, i2, tt, _, p2 = grp(g2)
                            upto(pe, tE, g2)
                            upto(pe, subd, g2, 1)
                            nc.tensor.matmul(S_[:, :], identb[:, :], mainb[:, tt, :, :], start=True, stop=False,
                                             skip_group_check=True)
                            for pr in range(2):
                                ins = nc.tensor.matmul(S_[:, pr * 2 * P:(pr + 1) * 2 * P], qT[:, p2, pr, :],
                                                       kz[:, i2, 2 * pr:2 * pr + 2, :], start=False, stop=True,
                                                       skip_group_check=True)
                            if tt == 1:
                                s4 = S_[0:WIN, :].rearrange("p (h k) -> p h k", h=HG)
                                for pr in range(2):
                                    nc.tensor.matmul(s4[:, 2 * pr:2 * pr + 2, P - WIN:P], qT[:, p2, pr, 0:WIN],
                                                     kz[:, i2 - GJ, 2 * pr:2 * pr + 2, P - WIN:P],
                                                     start=(pr == 0), stop=False, skip_group_check=True)
                                ins = nc.tensor.matmul(s4[:, :, P - WIN:P], identb[:, 0:WIN], prevb[:, :, :],
                                                       start=False, stop=True, skip_group_check=True)
                            ins.then_inc(simd, 1)
                        if g4 is not None and (live or g4[1] >= GB - 4):
                            _, _, _, _, p4 = grp(g4)
                            upto(pe, ond, g4)
                            if g2 is not None and (live or g2[1] >= GB - 2):
                                upto(pe, tE, g2)
                            for pr in range(2):
                                ins = nc.tensor.transpose(TB[:, pr * P:(pr + 1) * P],
                                                          on[:, p4, 2 * pr:2 * pr + 2, :], ident[:, :])
                            ins.then_inc(oTd, 1)
                        if g3 is not None and (live or g3[1] >= GB - 3):
                            _, i3, tt, _, p3 = grp(g3)
                            upto(pe, ptE, g3)
                            upto(pe, ond, g3, 1)
                            upto(pe, vE, g3)
                            for h in range(HG):
                                o = O_[:, h * (DH + 1):(h + 1) * (DH + 1)]
                                ins = nc.tensor.matmul(o, pT[:, tt, p3, h, :], vv[:, i3, h, :], start=True, stop=(tt == 0),
                                                       skip_group_check=True)
                                if tt == 1:
                                    ins = nc.tensor.matmul(o[0:WIN, :], pprev[:, p3, h, :], vv[:, i3 - GJ, h, :],
                                                           start=False, stop=True, skip_group_check=True)
                            ins.then_inc(pvd, 1)
                        if g4 is not None and (live or g4[1] >= GB - 4):
                            b4, _, tt, j4, p4 = grp(g4)
                            upto(pe, oTe, g4)
                            if tt == 0 and j4 == 0 and not (isinstance(b4, int) and b4 == 0):
                                pe.wait_ge(xup, b4 * 2)
                            for pr in range(2):
                                ins = nc.tensor.matmul(W_[:, tt * P:(tt + 1) * P], wo[:, (2 * j4 + pr) * P:(2 * j4 + pr + 1) * P],
                                                       oT[:, p4, pr, :], start=(j4 == 0 and pr == 0),
                                                       stop=(j4 == GJ - 1 and pr == 1), skip_group_check=True)
                            ins.then_inc(wod, 1)
                    pipeline(pe, slot, 4)

                @block.scalar
                def _(act):
                    def slot(g, live):
                        g2, g3, g4 = back(g, 2), back(g, 3), back(g, 4)
                        b, i, t, j, par = grp(g)
                        if g2 is not None and (live or g2[1] >= GB - 2):
                            _, i2, _, _, p2 = grp(g2)
                            upto(act, tT, g2)
                            upto(act, simd, g2, 2)
                            nc.scalar.activation(qT[:, p2, :, :], TB[:, 0:2 * P].rearrange("p (a n) -> p a n", a=2), ACT.Copy)
                            for e in range(2):
                                s = slice(64 * e, 64 * e + 64)
                                ins = nc.scalar.activation(kz[s, i2, e:HG:2, :],
                                                           TB[s, 2 * P:4 * P].rearrange("p (a n) -> p a n", a=2), ACT.Copy)
                            ins.then_inc(tE, 1)
                        if live:
                            upto(act, qkp, g)
                            upto(act, ssd, g, 2)
                            nc.scalar.activation(sq[:, par, :], A[par][:, :], ACT.Square).then_inc(sqd, 1)
                        if g3 is not None and (live or g3[1] >= GB - 3):
                            _, _, tt, _, p3 = grp(g3)
                            upto(act, ptT, g3)
                            upto(act, pvd, g3, 2)
                            src = PTB[:, :].rearrange("p (h q) -> p h q", h=HG)
                            if tt == 0:
                                ins = nc.scalar.activation(pT[:, 0, p3, :, :], src, ACT.Copy)
                            else:
                                nc.scalar.activation(pT[:, 1, p3, :, WIN:P], src[:, :, WIN:P], ACT.Copy)
                                nc.scalar.activation(pT[0:P - WIN, 1, p3, :, 0:WIN], src[0:P - WIN, :, 0:WIN], ACT.Copy)
                                ins = nc.scalar.activation(pprev[P - WIN:P, p3, :, :], src[P - WIN:P, :, 0:WIN], ACT.Copy)
                            ins.then_inc(ptE, 1)
                        if live:
                            upto(act, vp, g)
                            if t == 0:
                                upto(act, pvd, g, 4)
                            nc.scalar.activation(vv[:, i, :, 0:DH], V_[:, 0:HG * DH].rearrange("p (h c) -> p h c", h=HG),
                                                 ACT.Copy).then_inc(vE, 1)
                        if g4 is not None and (live or g4[1] >= GB - 4):
                            _, _, _, _, p4 = grp(g4)
                            upto(act, oTd, g4)
                            upto(act, wod, g4, 2)
                            nc.scalar.activation(oT[:, p4, :, :], TB[:, 0:2 * P].rearrange("p (a n) -> p a n", a=2),
                                                 ACT.Copy).then_inc(oTe, 1)
                        if g2 is not None and (live or g2[1] >= GB - 2):
                            _, _, _, _, p2 = grp(g2)
                            upto(act, subd, g2)
                            nc.scalar.activation(pb[:, p2, :, :], pb[:, p2, :, :], ACT.Exp).then_inc(expd, 1)
                    pipeline(act, slot, 4)

                @block.vector
                def _(dve):
                    def slot(g, live):
                        g2, g3, g4 = back(g, 2), back(g, 3), back(g, 4)
                        b, i, t, j, par = grp(g)
                        if live:
                            upto(dve, sqd, g)
                            upto(dve, qkd, g, 2)
                            nc.vector.tensor_tensor(t1[:, par, :], A[par][:, :],
                                                    tab[:, t, 0, :, :, :].rearrange("p a h c -> p (a h c)"), ALU.mult)
                            a3 = A[par][:, :].rearrange("p (h u c) -> p h u c", u=2, c=DH // 2)
                            o3 = t2[:, par, :].rearrange("p (h u c) -> p h u c", u=2, c=DH // 2)
                            s3 = tab[:, t, 1, :, :, :].rearrange("p a h (u c) -> p (a h) u c", u=2)
                            nc.vector.tensor_tensor(o3, a3[:, :, ::-1, :], s3, ALU.mult).then_inc(rot, 1)
                        if g2 is not None and (live or g2[1] >= GB - 2):
                            _, _, _, _, p2 = grp(g2)
                            s3 = S_[:, :].rearrange("p (h k) -> p h k", h=HG)
                            upto(dve, simd, g2)
                            nc.vector.tensor_reduce(mx[:, p2, :], s3, AX.X, ALU.max).then_inc(mxd, 1)
                            upto(dve, mxd, g2)
                            upto(dve, ptT, g2, 2)
                            nc.vector.tensor_tensor(pb[:, p2, :, :], s3, mx[:, p2, :].unsqueeze(2).to_broadcast([P, HG, P]),
                                                    ALU.subtract).then_inc(subd, 1)
                        if live:
                            upto(dve, prep, g, 2, 2)
                            nc.vector.tensor_reduce(ss[:, par, :], sq[:, par, :].rearrange("p (h c) -> p h c", c=DH),
                                                    AX.X, ALU.add).then_inc(ssd, 1)
                        if g3 is not None and (live or g3[1] >= GB - 3):
                            _, _, _, _, p3 = grp(g3)
                            o3 = O_[:, 0:HG * (DH + 1)].rearrange("p (h c) -> p h c", h=HG)
                            upto(dve, pvd, g3)
                            nc.vector.reciprocal(rd[:, p3, :], o3[:, :, DH]).then_inc(rdd, 1)
                            upto(dve, rdd, g3)
                            upto(dve, oTd, g3, 2)
                            nc.vector.tensor_tensor(on[:, p3, :, :], o3[:, :, 0:DH],
                                                    rd[:, p3, :].unsqueeze(2).to_broadcast([P, HG, DH]), ALU.mult).then_inc(ond, 1)
                        if g4 is not None and g4[1] == GB - 1:
                            b4 = g4[0]
                            upto(dve, wod, g4)
                            for lo, sh in ((0, 0), (64, 1)):
                                x = X[lo:lo + 64, bass.ds(b4 * XS + sh, T)]
                                nc.vector.tensor_tensor(x, W_[lo:lo + 64, 0:T], x, ALU.add).then_inc(xup, 1)
                    pipeline(dve, slot, 4)

                @block.gpsimd
                def _(pool):
                    def slot(g, live):
                        if not live:
                            return
                        b, i, _, _, par = grp(g)
                        if i == 1:
                            if not (isinstance(b, int) and b == 0):
                                pool.wait_ge(vp, b * GB)
                            nc.gpsimd.tensor_copy(xc[:, 1, :], X[:, bass.ds(b * XS + P, P)]).then_inc(xcd, 1)
                        if i == GJ + 1:
                            pool.wait_ge(vp, b * GB + GJ)
                            nc.gpsimd.tensor_copy(xc[:, 0, :], X[:, bass.ds((b + 1) * XS, P)]).then_inc(xcd, 1)
                        upto(pool, ssd, g)
                        upto(pool, rot, g)
                        nc.gpsimd.tensor_tensor(t1[:, par, :], t1[:, par, :], t2[:, par, :], ALU.add).then_inc(padd, 1)
                        nc.gpsimd.tensor_scalar(rn[:, par, :], ss[:, par, :], 1e-24, None, ALU.max).then_inc(prep, 1)
                        pool.wait_ge(prep, g[0] * (2 * GB) + (2 * g[1] + 1))
                        nc.gpsimd.tensor_tensor(rn[:, par, :], rn[:, par, :], mhalf[:, :], ALU.pow).then_inc(prep, 1)
                        upto(pool, prep, g, 0, 2)
                        upto(pool, padd, g)
                        upto(pool, tT, g, 2)
                        nc.gpsimd.tensor_tensor(qk[:, par, :].rearrange("p (h c) -> p h c", c=DH),
                                                t1[:, par, :].rearrange("p (h c) -> p h c", c=DH),
                                                rn[:, par, :].unsqueeze(2).to_broadcast([P, 8, DH]), ALU.mult).then_inc(qkd, 1)
                    nc.gpsimd.tensor_copy(xc[:, 0, :], X[:, 0:P]).then_inc(xcd, 1)
                    pipeline(pool, slot, 0)
            clear(nc, asems)

            def xs(c):
                return X[:, 2 * c * XS:(2 * c + 2) * XS].rearrange("p (b n) -> p b n", b=2)[:, :, 0:T]

            def two(ap):
                return ap.rearrange("p (b n) -> p b n", b=2)

            with nc.Block() as block:
                @block.sync
                def _(sp):
                    load_attention_weights(sp, wnext, layer + 1)
                    sp.wait_ge(wnext, 48)

                @block.gpsimd
                def _(pool):
                    pool.wait_ge(wnext, 48)
                    make_tables(pool, ftab)

                @block.tensor
                def _(pe):
                    for c in range(NC):
                        nc.tensor.matmul(two(bank[c][:, :]), avg[:, :], xs(c), start=True, stop=True).then_inc(fmean, 1)
                    for c in range(NC):
                        pe.wait_ge(fsq, c + 1)
                        nc.tensor.matmul(bank[4 + c][:, :], avg[:, :], sqf[:, c * CH:(c + 1) * CH],
                                         start=True, stop=True).then_inc(fvar, 1)

                    def up(c):
                        pe.wait_ge(fn2, c + 1)
                        if c == 0:
                            pe.wait_ge(frs, 2)
                        for k, (o, n) in enumerate(DB):
                            q = 3 * c + k
                            if q >= 3:
                                pe.wait_ge(fhd, q - 2)
                            g_, a_ = bank[2 * (q % 3)], bank[2 * (q % 3) + 1]
                            nc.tensor.matmul(g_[0:n, :], w1[:, DI + o:DI + o + n], rs[:, c * CH:(c + 1) * CH],
                                             start=True, stop=True)
                            nc.tensor.matmul(a_[0:n, :], w1[:, o:o + n], rs[:, c * CH:(c + 1) * CH],
                                             start=True, stop=True).then_inc(fgp, 1)

                    def down(c):
                        if c >= 2:
                            pe.wait_ge(fx, 4 * (c - 1))
                        elif c == 0:
                            pe.wait_ge(frs, NC)
                        for k, (o, n) in enumerate(DB):
                            pe.wait_ge(fhd, 3 * c + k + 1)
                            ins = nc.tensor.matmul(bank[6 + c % 2][:, :], w2[0:n, k * P:(k + 1) * P], hh[0:n, c % 2, k, :],
                                                   start=(k == 0), stop=(k == 2))
                        ins.then_inc(fy, 1)
                    up(0)
                    for c in range(1, NC):
                        up(c)
                        down(c - 1)
                    down(NC - 1)

                @block.scalar
                def _(act):
                    for c in range(NC):
                        s = slice(c * CH, (c + 1) * CH)
                        act.wait_ge(fdev, c + 1)
                        nc.scalar.activation(sqf[:, s], dev[:, s], ACT.Square).then_inc(fsq, 1)
                    for c in range(NC):
                        s = slice(c * CH, (c + 1) * CH)
                        act.wait_ge(fvar, c + 1)
                        nc.scalar.activation(sqf[:, s], bank[4 + c][:, :], ACT.Ln, bias=eps[:, 0:1]).then_inc(flog, 1)
                        act.wait_ge(flog, c + 1)
                        nc.scalar.activation(rs[:, s], sqf[:, s], ACT.Exp, scale=-0.5).then_inc(frs, 1)
                    for c in range(NC):
                        for k, (o, n) in enumerate(DB):
                            q = 3 * c + k
                            act.wait_ge(fgp, q + 1)
                            if q >= 6:
                                act.wait_ge(fhd, q - 5)
                            nc.scalar.activation(gl[0:n, c % 2, k, :], bank[2 * (q % 3)][0:n, :], ACT.Gelu,
                                                 bias=fv[0:n, 6 + k:7 + k]).then_inc(fgd, 1)

                @block.vector
                def _(dve):
                    for c in range(NC):
                        dve.wait_ge(fmean, c + 1)
                        nc.vector.tensor_tensor(two(dev[:, c * CH:(c + 1) * CH]), xs(c), two(bank[c][:, :]),
                                                ALU.subtract).then_inc(fdev, 1)
                    for c in range(NC):
                        s = slice(c * CH, (c + 1) * CH)
                        dve.wait_ge(frs, c + 1)
                        nc.vector.tensor_tensor(rs[:, s], dev[:, s], rs[:, s], ALU.mult).then_inc(fn1, 1)
                        dve.wait_ge(fn1, c + 1)
                        nc.vector.tensor_scalar(rs[:, s], rs[:, s], fv[:, 0:1], fv[:, 1:2], ALU.mult, ALU.add).then_inc(fn2, 1)

                    def gate(c):
                        for k, (o, n) in enumerate(DB):
                            q = 3 * c + k
                            dve.wait_ge(fgd, q + 1)
                            if c >= 2 and k == 0:
                                dve.wait_ge(fy, c - 1)
                            nc.vector.scalar_tensor_tensor(out=hh[0:n, c % 2, k, :], in0=bank[2 * (q % 3) + 1][0:n, :],
                                                           scalar=fv[0:n, 3 + k:4 + k], in1=gl[0:n, c % 2, k, :],
                                                           op0=ALU.add, op1=ALU.mult).then_inc(fhd, 1)

                    def update(c):
                        dve.wait_ge(fy, c + 1)
                        for u in range(2):
                            for lo, sh in ((0, 0), (64, 1)):
                                b = 2 * c + u
                                x = X[lo:lo + 64, b * XS + sh:b * XS + sh + T]
                                nc.vector.scalar_tensor_tensor(out=x, in0=bank[6 + c % 2][lo:lo + 64, u * T:(u + 1) * T],
                                                               scalar=fv[lo:lo + 64, 2:3], in1=x,
                                                               op0=ALU.add, op1=ALU.add).then_inc(fx, 1)
                    gate(0)
                    for c in range(1, NC):
                        gate(c)
                        update(c - 1)
                    update(NC - 1)
            clear(nc, fsems)
        clear(nc, isems)


def fire_attention_phase(nc, res, d, M, XN):
    bank, ident = res["bank"], res["ident"]
    C = 3 * P
    GA, GT = 12, 4
    RM = T + 4 * (T // 4 - 1)
    ROFF = RM - T
    with ExitStack() as ctx:
        phase = res["phase"] = res["phase"] + 1

        def sb(name, shape, dt=FP32):
            return ctx.enter_context(nc.sbuf_tensor(f"{name}_{phase}", shape, dt))

        def sem(name):
            s = ctx.enter_context(nc.semaphore(f"{name}_{phase}"))
            sems.append(s)
            return s
        sems = []
        wqkv, wp = sb("fa_wqkv", [P, C]), sb("fa_wp", [P, P])
        bqk, bv = sb("fa_bqk", [P, 3]), sb("fa_bv", [P, P])
        sc = sb("fa_sc", [P, 4])
        wb = sb("fa_wb", [P, 2])
        w2 = sb("fa_w2", [P, 4 * NH])
        b2 = sb("fa_b2", [P, NH])
        hmask = sb("fa_hmask", [P, NH])
        rel = sb("fa_rel", [P, RM])
        pn = sb("fa_pn", [P, T])
        nd = sb("fa_nd", [P, 8, T])
        hb = sb("fa_hb", [P, 8, T])
        bias = [sb("fa_bias0", [P, NH, P]), sb("fa_bias1", [P, NH, T])]
        xb = sb("fa_xb", [P, T])
        qT = sb("fa_qT", [P, 2, T])
        kz = sb("fa_kz", [P, 2, NH, T])
        vv = sb("fa_vv", [P, 2, 2, NH, HD + 1])
        S = sb("fa_S", [P, 4, 512])
        mx = sb("fa_mx", [P, 4, 4])
        pT = sb("fa_pT", [P, 2, 4, P])
        rd = sb("fa_rd", [P, 2, NH])
        on = sb("fa_on", [P, 2, P])
        oT = sb("fa_oT", [P, P])
        ysb = sb("fa_ysb", [P, 2, P])
        ld, zd, ach, vch = sem("fa_ld"), sem("fa_zd"), sem("fa_ach"), sem("fa_vch")
        ndd, hd_, bp, be = sem("fa_ndd"), sem("fa_hd"), sem("fa_bp"), sem("fa_be")
        SCALE = float(np.float32(1.0) / np.sqrt(np.float32(HD)))

        with nc.Block() as block:
            @block.sync
            def _(sp):
                for dst, src in ((wqkv[:, :], d["fa_wqkv"]), (wp[:, :], d["fa_wp"]), (bqk[:, :], d["fa_bqk"]),
                                 (bv[:, :], d["fa_bv"].to_broadcast([P, P])), (b2[:, :], d["fa_b2"].to_broadcast([P, NH])),
                                 (sc[:, 0:2], d["fa_sc"].to_broadcast([P, 2])), (wb[:, :], d["fa_wb"]),
                                 (hmask[:, :], d["c_hmask"]), (rel[:, :], d["c_rel"]), (pn[:, :], d["c_pos"])):
                    sp.dma_start(dst, src).then_inc(ld, 16)
                sp.wait_ge(zd, 1)
                for g in range(4):
                    sp.dma_start(w2[g * BW:(g + 1) * BW, g * NH:(g + 1) * NH], d["fa_w2"]).then_inc(ld, 16)
                sp.wait_ge(ld, 16 * 14)

            @block.gpsimd
            def _(pool):
                nc.gpsimd.memset(w2[:, :], 0.0).then_inc(zd, 1)
                nc.gpsimd.memset(vv[:, :, :, :, :], 1.0)

            @block.scalar
            def _(act):
                act.wait_ge(ld, 16 * 14)
                nc.scalar.activation(sc[:, 2:3], sc[:, 1:2], ACT.Abs, scale=INIT_L).then_inc(ach, 1)
                nc.scalar.activation(rel[:, :], rel[:, :], ACT.Abs, scale=sc[:, 0:1]).then_inc(ach, 1)
                act.wait_ge(vch, 1)
                nc.scalar.activation(pn[:, :], pn[:, :], ACT.Abs, scale=sc[:, 0:1]).then_inc(ach, 1)
                act.wait_ge(ach, 3)
                nc.scalar.activation(rel[:, :], rel[:, :], ACT.Ln, bias=1.0).then_inc(ach, 1)
                nc.scalar.activation(pn[:, :], pn[:, :], ACT.Ln, bias=1.0).then_inc(ach, 1)

            @block.vector
            def _(dve):
                dve.wait_ge(ach, 1)
                nc.vector.tensor_scalar(pn[:, :], pn[:, :], sc[:, 2:3], None, ALU.max).then_inc(vch, 1)
                nc.vector.tensor_scalar(sc[:, 3:4], bqk[:, 0:1], SCALE, None, ALU.mult)
                dve.wait_ge(ach, 5)
                nc.vector.tensor_scalar(pn[:, :], pn[:, :], 1e-6, None, ALU.add).then_inc(vch, 1)
                dve.wait_ge(vch, 2)
                nc.vector.reciprocal(pn[:, :], pn[:, :])

        with nc.Block() as block:
            def rounds(eng, body):
                body(0, 2)
                with eng.Fori(1, 4) as r:
                    body(r, 2)
                with eng.Fori(4, 8) as r:
                    body(r, 1)

            @block.vector
            def _(dve):
                def distances(r, tiles):
                    if not isinstance(r, int):
                        dve.wait_ge(hd_, r)
                    for i in range(8):
                        ins = nc.vector.tensor_tensor(nd[:, i, :], rel[:, bass.ds(r * -32 + (ROFF - 4 * i), T)]
                                                      if not isinstance(r, int) else rel[:, ROFF - 4 * i:ROFF - 4 * i + T],
                                                      pn[:, :], ALU.mult)
                    ins.then_inc(ndd, 1)

                def evacuate(r, tiles):
                    dve.wait_ge(bp, r + 1)
                    for t in range(2 - tiles, 2):
                        ins = nc.vector.tensor_tensor(bias[t][:, :, bass.ds(r * 32, 32)],
                                                      bank[t][:, :].rearrange("p (s h) -> p h s", h=NH),
                                                      b2[:, :].unsqueeze(2).to_broadcast([P, NH, 32]), ALU.add)
                    ins.then_inc(be, 1)

                def body(r, tiles):
                    distances(r, tiles)
                    evacuate(r, tiles)
                rounds(dve, body)

            @block.scalar
            def _(act):
                def body(r, tiles):
                    act.wait_ge(ndd, r + 1)
                    if not isinstance(r, int):
                        act.wait_ge(bp, r)
                    nc.scalar.activation(hb[:, :, :], nd[:, :, :], ACT.Relu, scale=wb[:, 0:1], bias=wb[:, 1:2]).then_inc(hd_, 1)
                rounds(act, body)

            @block.tensor
            def _(pe):
                def body(r, tiles):
                    pe.wait_ge(hd_, r + 1)
                    if not isinstance(r, int):
                        pe.wait_ge(be, r)
                    for t in range(2 - tiles, 2):
                        for i in range(8):
                            ins = nc.tensor.matmul(bank[t][:, i * 4 * NH:(i + 1) * 4 * NH], hb[:, i, t * P:(t + 1) * P],
                                                   w2[:, :], start=True, stop=True, skip_group_check=True)
                    ins.then_inc(bp, 1)
                rounds(pe, body)

            @block.gpsimd
            def _(pool):
                pool.wait_ge(be, 8)
                for t in range(2):
                    n = (t + 1) * P
                    nc.gpsimd.affine_select(out=bias[t][:, :, :], in_=bias[t][:, :, :], compare_op=ALU.is_ge, fill=-BIG,
                                            base=t * P, pattern=[[0, NH], [-1, n]], channel_multiplier=1)

        simd, addd, mxd, subd, expd = [sem("fa_" + n) for n in ("simd", "addd", "mxd", "subd", "expd")]
        ptT, ptE, pvd = [sem("fa_" + n) for n in ("ptT", "ptE", "pvd")]
        xbd, projd, qE, kzd, vE = [sem("fa_" + n) for n in ("xbd", "projd", "qE", "kzd", "vE")]
        rdd, ond, oTd, oTe, yd, yE, upd = [sem("fa_" + n) for n in ("rdd", "ond", "oTd", "oTe", "yd", "yE", "upd")]
        SIM, PTR, PVS, OTR, YPR = 4, 6, 7, 8, 9
        G2 = 2 * GA

        def back(g, k):
            b, i = g
            i -= k
            while i < 0:
                b, i = b - 1, i + G2
            return None if isinstance(b, int) and b < 0 else (b, i)

        def upto(eng, s, q):
            if q is not None:
                eng.wait_ge(s, q[0] * G2 + (q[1] + 1))

        def info(q):
            par, i = q[1] // GA, q[1] % GA
            return (par, 0, 4 * i, 4, P) if i < GT else (par, 1, 2 * (i - GT), 2, T)

        def tile_end(q):
            if q is None or q[1] % GA not in (GT - 1, GA - 1):
                return None
            return q[0], 2 * (q[1] // GA) + (q[1] % GA == GA - 1)

        def upto_tile(eng, s, tl, k=0):
            if isinstance(tl[0], int) and tl[0] * 4 + tl[1] - k < 0:
                return
            eng.wait_ge(s, tl[0] * 4 + (tl[1] - k + 1))

        def pipeline(eng, slot):
            for i in range(G2):
                slot((0, i), True)
            with eng.Fori(1, B // 2) as b:
                for i in range(G2):
                    slot((b, i), True)
            for i in range(YPR + 1):
                slot((B // 2, i), False)

        def at(g, k, live):
            q = back(g, k)
            return q if q is not None and (live or q[0] == B // 2 - 1 and isinstance(q[0], int)) else None

        with nc.Block() as block:
            @block.gpsimd
            def _(pool):
                def slot(g, live):
                    if live and g[1] % GA == 0:
                        par = g[1] // GA
                        if par or not isinstance(g[0], int):
                            pool.wait_ge(projd, g[0] * 4 + 2 * par)
                        nc.gpsimd.tensor_copy(xb[:, :], XN[:, bass.ds(g[0] * (2 * T) + par * T, T)]).then_inc(xbd, 1)
                    q = at(g, SIM, live)
                    if q is not None:
                        _, _, _, nh, nk = info(q)
                        s = S[:, q[1] % 4, :].rearrange("p (h k) -> p h k", h=nh)
                        upto(pool, mxd, q)
                        nc.gpsimd.tensor_tensor(s, s, mx[:, q[1] % 4, 0:nh].unsqueeze(2).to_broadcast([P, nh, nk]),
                                                ALU.subtract).then_inc(subd, 1)
                pipeline(pool, slot)

            @block.tensor
            def _(pe):
                def slot(g, live):
                    if live and g[1] % GA == 1:
                        par = g[1] // GA
                        pe.wait_ge(xbd, g[0] * 2 + (par + 1))
                        if par or not isinstance(g[0], int):
                            pe.wait_ge(kzd, (g[0] * 2 + par) * 4)
                            pe.wait_ge(vE, g[0] * 2 + par)
                        for w in range(2):
                            ins = nc.tensor.matmul(bank[6][:, w * T:(w + 1) * T], wqkv[:, w * P:(w + 1) * P], xb[:, :],
                                                   start=True, stop=True, skip_group_check=True)
                        ins.then_inc(projd, 1)
                        for t in range(2):
                            ins = nc.tensor.matmul(bank[7][:, t * P:(t + 1) * P], xb[:, t * P:(t + 1) * P], wqkv[:, 2 * P:3 * P],
                                                   start=True, stop=True, skip_group_check=True)
                        ins.then_inc(projd, 1)
                    q = at(g, PTR, live)
                    if q is not None:
                        upto(pe, expd, q)
                        upto(pe, ptE, back(q, 2))
                        for h in range(4):
                            ins = nc.tensor.transpose(bank[2 + q[1] % 2][:, h * P:(h + 1) * P],
                                                      S[:, q[1] % 4, h * P:(h + 1) * P], ident[:, :])
                        ins.then_inc(ptT, 1)
                    q = at(g, SIM, live)
                    if q is not None:
                        par, t, h0, nh, nk = info(q)
                        if q[1] % GA < GT:
                            pe.wait_ge(kzd, q[0] * 8 + (par * 4 + q[1] % GA + 1))
                        upto(pe, addd, back(q, 2))
                        nc.tensor.matmul(bank[q[1] % 2][:, :].rearrange("p (h k) -> p h k", h=nh),
                                         qT[:, par, t * P:(t + 1) * P], kz[:, par, h0:h0 + nh, 0:nk],
                                         start=True, stop=True).then_inc(simd, 1)
                    q = at(g, YPR, live)
                    tl = tile_end(q)
                    if tl is not None:
                        upto_tile(pe, oTe, tl)
                        nc.tensor.matmul(bank[5][:, 0:P], wp[:, :], oT[:, :], start=True, stop=True).then_inc(yd, 1)
                    q = at(g, OTR, live)
                    tl = tile_end(q)
                    if tl is not None:
                        upto_tile(pe, ond, tl)
                        upto_tile(pe, yE, tl, 1)
                        nc.tensor.transpose(bank[5][:, 0:P], on[:, tl[1] % 2, :], ident[:, :]).then_inc(oTd, 1)
                    q = at(g, PVS, live)
                    if q is not None:
                        par, t, h0, nh, nk = info(q)
                        upto(pe, ptE, q)
                        first = q[1] % GA in (0, GT)
                        if first:
                            tb = tile_end((q[0], q[1] - q[1] % GA + (GT - 1 if t == 0 else GA - 1)))
                            upto_tile(pe, ond, tb, 1)
                            pe.wait_ge(vE, q[0] * 2 + (par + 1))
                        for k in range(nh):
                            o = bank[4][:, (h0 + k) * (HD + 1):(h0 + k + 1) * (HD + 1)]
                            for kt in range(t + 1):
                                ins = nc.tensor.matmul(o, pT[:, q[1] % 2, k * (t + 1) + kt, :], vv[:, par, kt, h0 + k, :],
                                                       start=(kt == 0), stop=(kt == t), skip_group_check=True)
                        ins.then_inc(pvd, 1)
                pipeline(pe, slot)

            @block.scalar
            def _(act):
                def slot(g, live):
                    if live and g[1] % GA == 1:
                        par = g[1] // GA
                        act.wait_ge(projd, g[0] * 4 + (2 * par + 1))
                        nc.scalar.activation(qT[:, par, :], bank[6][:, 0:T], ACT.Identity, bias=sc[:, 3:4],
                                             scale=SCALE).then_inc(qE, 1)
                    q = at(g, PTR, live)
                    if q is not None:
                        upto(act, ptT, q)
                        upto(act, pvd, back(q, 2))
                        nc.scalar.activation(pT[:, q[1] % 2, :, :], bank[2 + q[1] % 2][:, :].rearrange("p (h q) -> p h q", h=4),
                                             ACT.Copy).then_inc(ptE, 1)
                    q = at(g, SIM, live)
                    if q is not None:
                        upto(act, subd, q)
                        s = S[:, q[1] % 4, :]
                        nc.scalar.activation(s, s, ACT.Exp).then_inc(expd, 1)
                    tl = tile_end(at(g, OTR, live))
                    if tl is not None:
                        upto_tile(act, oTd, tl)
                        nc.scalar.activation(oT[:, :], bank[5][:, 0:P], ACT.Copy).then_inc(oTe, 1)
                    tl = tile_end(at(g, YPR, live))
                    if tl is not None:
                        upto_tile(act, yd, tl)
                        upto_tile(act, upd, tl, 2)
                        nc.scalar.activation(ysb[:, tl[1] % 2, :], bank[5][:, 0:P], ACT.Identity, bias=bqk[:, 2:3]).then_inc(yE, 1)
                pipeline(act, slot)

            @block.vector
            def _(dve):
                def slot(g, live):
                    i, par = g[1] % GA, g[1] // GA
                    if live and i == 1:
                        dve.wait_ge(projd, g[0] * 4 + (2 * par + 2))
                        nc.vector.tensor_tensor(vv[:, par, :, :, 0:HD],
                                                bank[7][:, 0:T].rearrange("p (t h c) -> p t h c", t=2, h=NH),
                                                bv[:, :].rearrange("p (h c) -> p h c", h=NH).unsqueeze(1)
                                                .to_broadcast([P, 2, NH, HD]), ALU.add).then_inc(vE, 1)
                    if live and 2 <= i < 6:
                        h0 = 4 * (i - 2)
                        if i == 2:
                            dve.wait_ge(qE, g[0] * 2 + (par + 1))
                        nc.vector.scalar_tensor_tensor(out=kz[:, par, h0:h0 + 4, :],
                                                       in0=bank[6][:, T:2 * T].unsqueeze(1).to_broadcast([P, 4, T]),
                                                       scalar=bqk[:, 1:2],
                                                       in1=hmask[:, h0:h0 + 4].unsqueeze(2).to_broadcast([P, 4, T]),
                                                       op0=ALU.add, op1=ALU.mult).then_inc(kzd, 1)
                    q = at(g, SIM, live)
                    if q is not None:
                        _, t, h0, nh, nk = info(q)
                        s = S[:, q[1] % 4, :].rearrange("p (h k) -> p h k", h=nh)
                        upto(dve, simd, q)
                        upto(dve, ptT, back(q, 4))
                        nc.vector.tensor_tensor(s, bank[q[1] % 2][:, :].rearrange("p (h k) -> p h k", h=nh),
                                                bias[t][:, h0:h0 + nh, :], ALU.add).then_inc(addd, 1)
                        upto(dve, addd, q)
                        nc.vector.tensor_reduce(mx[:, q[1] % 4, 0:nh], s, AX.X, ALU.max).then_inc(mxd, 1)
                    q = at(g, PVS, live)
                    tl = tile_end(q)
                    if tl is not None:
                        o = bank[4][:, 0:NH * (HD + 1)].rearrange("p (h c) -> p h c", h=NH)
                        upto(dve, pvd, q)
                        nc.vector.reciprocal(rd[:, tl[1] % 2, :], o[:, :, HD]).then_inc(rdd, 1)
                        upto_tile(dve, rdd, tl)
                        upto_tile(dve, oTd, tl, 2)
                        nc.vector.tensor_tensor(on[:, tl[1] % 2, :].rearrange("p (h c) -> p h c", h=NH), o[:, :, 0:HD],
                                                rd[:, tl[1] % 2, :].unsqueeze(2).to_broadcast([P, NH, HD]),
                                                ALU.mult).then_inc(ond, 1)
                    tl = tile_end(at(g, YPR, live))
                    if tl is not None:
                        m = M[:, bass.ds(tl[0] * (4 * P) + tl[1] * P, P)]
                        upto_tile(dve, yE, tl)
                        nc.vector.tensor_tensor(m, m, ysb[:, tl[1] % 2, :], ALU.add).then_inc(upd, 1)
                pipeline(dve, slot)
        clear(nc, sems)


def program(nc, d, out, stop):
    with ExitStack() as ctx:
        def sb(name, shape, dt=FP32):
            return ctx.enter_context(nc.sbuf_tensor(name, shape, dt))
        bank = [ctx.enter_context(nc.psum_tensor(f"bank{i}", [P, 512], FP32)) for i in range(8)]
        M = sb("M", [P, NT])
        XN = sb("XN", [P, NT])
        X = sb("X", [P, (B + 1) * XS])
        ident = sb("ident", [P, P])
        identb = sb("identb", [P, P], BF16)
        avg = sb("avg", [P, P])
        eps = sb("eps", [P, 1])
        mhalf = sb("mhalf", [P, 8])
        rank = sb("rank", [P, TILES, EXPERTS])
        rot = sb("rot", [P, 8 * DH])
        mainf = sb("mainf", [P, 2, P])
        prevf = sb("prevf", [P, WIN])
        mainb = sb("mainb", [P, 2, HG, P], BF16)
        prevb = sb("prevb", [P, HG, WIN], BF16)
        start_ld = ctx.enter_context(nc.semaphore("start_ld"))
        out_st = ctx.enter_context(nc.semaphore("out_st"))
        res = dict(bank=bank, ident=ident, identb=identb, avg=avg, eps=eps, mhalf=mhalf, rank=rank, rot=rot,
                   mainb=mainb, prevb=prevb, phase=0)

        with nc.Block() as block:
            @block.sync
            def _(sp):
                for dst, src in ((M[:, :], d["x"]), (ident[:, :], d["c_ident"]), (rot[:, :], d["c_rot"]),
                                 (mainf[:, :, :], d["c_main"]), (prevf[:, :], d["c_prev"]),
                                 (rank[:, :, :].rearrange("p t e -> p (t e)"), d["c_rank"])):
                    sp.dma_start(dst, src).then_inc(start_ld, 16)
                sp.wait_ge(start_ld, 16 * 6)

            @block.gpsimd
            def _(pool):
                nc.gpsimd.memset(avg[:, :], 1.0 / P)
                nc.gpsimd.memset(eps[:, :], EPS)
                nc.gpsimd.memset(mhalf[:, :], -0.5)
                nc.gpsimd.memset(X[:, :], 0.0)

            @block.vector
            def _(dve):
                dve.wait_ge(start_ld, 16 * 6)
                nc.vector.tensor_copy(identb[:, :], ident[:, :])
                for t in range(2):
                    nc.vector.tensor_copy(mainb[:, t, :, :], mainf[:, t, :].unsqueeze(1).to_broadcast([P, HG, P]))
                nc.vector.tensor_copy(prevb[:, :, :], prevf[:, :].unsqueeze(1).to_broadcast([P, HG, WIN]))

        def run():
            layer_norm_block(nc, res, M, plain(XN))
            moe_phase(nc, res, d, M, XN)
            if stop == 1:
                return
            layer_norm_block(nc, res, M, plain(XN))
            recurrence_phase(nc, res, d, M, XN)
            if stop == 2:
                return
            layer_norm_block(nc, res, M, plain(XN))
            moe_phase(nc, res, d, M, XN)
            layer_norm_block(nc, res, M, shifted(X))
            local_transformer_phase(nc, res, d, X, 0)
            layer_norm_block(nc, res, M, plain(XN), add_shifted=X)
            if stop == 3:
                return
            fire_attention_phase(nc, res, d, M, XN)
            if stop == 4:
                return
            layer_norm_block(nc, res, M, shifted(X))
            local_transformer_phase(nc, res, d, X, 1)
            layer_norm_block(nc, res, M, plain(XN), add_shifted=X)
        run()
        with nc.Block() as block:
            @block.sync
            def _(sp):
                sp.dma_start(out, M[:, :]).then_inc(out_st, 16)
                sp.wait_ge(out_st, 16)


def rotary_constants():
    f = np.float32
    half = np.arange(0, DH, 2, dtype=f)
    inv_freq = (f(1.0) / np.power(f(10000.0), half / f(DH))).astype(f)
    t = np.arange(T, dtype=f)
    freqs = t[:, None] * inv_freq[None, :]
    base = (half + f(0.4 * DH)) / f(1.4 * DH)
    power = (t - f(T // 2)) / f(WIN // 2)
    scale = np.power(base[None, :], power[:, None]).astype(f)
    cos, sin = np.cos(freqs), np.sin(freqs)
    c2 = np.concatenate([cos, cos], -1)
    s2 = np.concatenate([-sin, sin], -1)
    sc = np.concatenate([scale, scale], -1)
    tab = np.stack([np.stack([f(8.0) * c2 * sc, c2 / sc], 1), np.stack([f(8.0) * s2 * sc, s2 / sc], 1)], 1)
    return tab.reshape(2, P, 2, 2, DH).transpose(1, 0, 2, 3, 4).reshape(P, 8 * DH).astype(f)


def mask_constants():
    q, k = np.arange(P)[:, None], np.arange(P)[None, :]
    own = (q // WIN == k // WIN) & (k <= q)
    prev = (q // WIN == k // WIN + 1) & (k % WIN >= q % WIN)
    m = np.where(own | prev, 0.0, -BIG).astype(np.float32)
    main = np.stack([m, m], 1)
    qi, kj = np.arange(P)[:, None], np.arange(WIN)[None, :]
    pv = np.where((kj >= qi) | (qi >= WIN), 0.0, -BIG).astype(np.float32)
    return main.reshape(P, 2 * P), pv


STOP = 0


def kernel(**inputs):
    import numpy as _np
    import concourse.bacc as _bacc
    from concourse import mybir as _mybir
    from concourse.bass_utils import run_bass_kernel_spmd as _run

    g = {k: _np.asarray(v) for k, v in inputs.items()}
    main, prev = mask_constants()
    a = {"x": g["L0_attn_x"].reshape(NT, P).T}
    a["moe_wr"] = g["L0_ffn_Wr"].T
    a["moe_w1"] = g["L0_ffn_W1"].transpose(0, 2, 1)
    a["moe_w2"] = g["L0_ffn_W2"].reshape(EXPERTS, P, FB, P).transpose(0, 3, 2, 1).reshape(EXPERTS, P, FFN)
    a["moe_bb"] = _np.concatenate([g["L0_ffn_b1"].reshape(EXPERTS, FB, P), g["L0_ffn_b2"][:, None]], 1).transpose(0, 2, 1)
    a["rg_win"], a["rg_wa"] = g["L0_attn_w_in"], g["L0_attn_w_a"]
    a["rg_vec"] = _np.stack([g["L0_attn_b_in"].reshape(P), g["L0_attn_b_a"].reshape(P), g["L0_attn_a_param"]], 1)
    w = g["L1_ffn_Wqkv"].reshape(DEPTH, P, 3, GJ, HG * DH).transpose(0, 1, 3, 2, 4).reshape(DEPTH, P, 3 * INNER)
    a["lt_wqkv"] = _np.concatenate([w, w[:1]])
    w = g["L1_ffn_Wo"].reshape(DEPTH, INNER // P, P, P).transpose(0, 2, 1, 3).reshape(DEPTH, P, INNER)
    a["lt_wo"] = _np.concatenate([w, w[:1]])
    q, k = g["L1_ffn_q_scale"], g["L1_ffn_k_scale"]
    w = _np.concatenate([q, k, _np.roll(q, DH // 2, 1), _np.roll(k, DH // 2, 1)], 1)
    a["lt_qs"] = _np.concatenate([w, w[:1]])
    a["lt_w1"] = g["L1_ffn_W1"]
    pad = 3 * P - DI
    a["lt_w2"] = _np.pad(g["L1_ffn_W2"], ((0, 0), (0, pad), (0, 0))).reshape(DEPTH, 3, P, P).transpose(0, 2, 1, 3).reshape(DEPTH, P, 3 * P)
    b1 = _np.pad(g["L1_ffn_b1"].reshape(DEPTH, 2, DI), ((0, 0), (0, 0), (0, pad))).reshape(DEPTH, 6, P)
    a["lt_fv"] = _np.concatenate([g["L1_ffn_ln_g"][:, None], g["L1_ffn_ln_b"][:, None], g["L1_ffn_b2"][:, None], b1],
                                 1).transpose(0, 2, 1)
    a["c_ident"] = _np.eye(P, dtype=_np.float32)
    a["c_rot"] = rotary_constants()
    a["c_main"], a["c_prev"] = main, prev
    a["c_rank"] = _np.tile(_np.arange(EXPERTS, 0, -1, dtype=_np.float32), (P, TILES))
    a["fa_wqkv"], a["fa_wp"] = g["L1_attn_Wqkv"], g["L1_attn_Wproj"]
    a["fa_bqk"] = _np.stack([g["L1_attn_bqkv"][:P], g["L1_attn_bqkv"][P:2 * P], g["L1_attn_bproj"]], 1)
    a["fa_bv"], a["fa_b2"] = g["L1_attn_bqkv"][None, 2 * P:], g["L1_attn_b2"][None]
    a["fa_sc"] = _np.stack([g["L1_attn_c_param"].reshape(()), g["L1_attn_L_multiplier"].reshape(())])[None]
    a["fa_wb"] = _np.tile(_np.stack([g["L1_attn_w1"][0], g["L1_attn_b1"]], 1), (4, 1))
    a["fa_w2"] = g["L1_attn_w2"]
    part = _np.arange(P)[:, None]
    a["c_hmask"] = (part // HD == _np.arange(NH)[None, :]).astype(_np.float32)
    ndist = 2 * T - 4
    a["c_rel"] = (_np.arange(ndist)[None, :] - (ndist - T) - part // BW).astype(_np.float32)
    a["c_pos"] = _np.tile(_np.arange(T, dtype=_np.float32), (P, 1))

    nc = _bacc.Bacc("TRN2", target_bir_lowering=False, num_devices=1)
    arrays, d = {}, {}
    for name, v in a.items():
        v = _np.ascontiguousarray(v)
        arrays["in_" + name] = v
        d[name] = nc.dram_tensor("in_" + name, v.shape, _mybir.dt.from_np(v.dtype), kind="ExternalInput").ap()
    d["comb_scratch"] = nc.dram_tensor("comb_scratch", (EXPERTS, NT), _mybir.dt.float32, kind="Internal").ap()
    out = nc.dram_tensor("out_x", (P, NT), _mybir.dt.float32, kind="ExternalOutput").ap()
    program(nc, d, out, STOP)
    r = _run(nc, [arrays], core_ids=[0])
    return _np.ascontiguousarray(r.results[0]["out_x"].T).reshape(B, T, P)
```
